# Optimizing a Trainium2 kernel written in Bass

```python
import numpy as np
import jax
import jax.numpy as jnp

def _softmax(x, axis=-1):
    return jax.nn.softmax(x, axis=axis)

def _gelu(x):
    return jax.nn.gelu(x, approximate=True)

def _silu(x):
    return jax.nn.silu(x)

def _sigmoid(x):
    return jax.nn.sigmoid(x)

def _layernorm(x, axis=-1, eps=1e-05):
    m = jnp.mean(x, axis=axis, keepdims=True)
    v = jnp.var(x, axis=axis, keepdims=True)
    return (x - m) / jnp.sqrt(v + eps)

def _scatter_add(tgt, idx, src, axis=0):
    return tgt.at[idx].add(src)

def _segment_sum(src, seg, n):
    return jax.ops.segment_sum(src, seg, n)
kernel_name = 'mk_xattn_ffn_d1_seqx_r4_97787a'

def setup_inputs(seed: int=0):
    np.random.seed(seed)
    _w = jnp.asarray

    def _rec_inputs():
        import jax
        import jax.numpy as jnp
        _rk = jax.random.key(seed)
        x = 7.22e-05 + 1 * jax.random.normal(jax.random.fold_in(_rk, 1), (8, 256, 256), jnp.float32)
        _lenS = 256 - jax.random.randint(jax.random.fold_in(_rk, 7), (8,), 0, max(1, 256 // 4) + 1, jnp.int32)
        _lenS2 = 77 - jax.random.randint(jax.random.fold_in(_rk, 8), (8,), 0, max(1, 77 // 4) + 1, jnp.int32)
        _ctx_768P = jax.random.normal(jax.random.fold_in(_rk, 11), (8, 16, 192), jnp.float32)
        _ctx_768c = jax.random.dirichlet(jax.random.fold_in(_rk, 511), 0.3 * jnp.ones((16,), jnp.float32), (8, 77))
        _ctx_768t = jnp.einsum('bsk,bkd->bsd', _ctx_768c, _ctx_768P)
        _ctx_768t = _ctx_768t * jax.lax.rsqrt(jnp.mean(jnp.square(_ctx_768t)) + 1e-12) * 0.953939
        ctx_768 = -0.000191848 + 0.999787 * (_ctx_768t + 0.3 * jax.random.normal(jax.random.fold_in(_rk, 611), (8, 77, 192), jnp.float32))
        return (x, ctx_768)
    x, ctx_768 = _rec_inputs()

    def _L0_xattn_setup():
        import math
        import jax, jax.numpy as jnp
        import numpy as np
        B, SQ, SKV = (4, 512, 512)
        D_EMBED, D_CROSS, D_ATT, N_HEADS = (256, 192, 256, 16)
        D_HEAD = D_ATT // N_HEADS

        def _split_heads(t):
            b, s, _ = t.shape
            return t.reshape(b, s, N_HEADS, D_HEAD).transpose(0, 2, 1, 3)
        key = jax.random.key(seed)
        ks = jax.random.split(key, 10)
        s_e = 1.0 / math.sqrt(D_EMBED)
        s_c = 1.0 / math.sqrt(D_CROSS)
        s_a = 1.0 / math.sqrt(D_ATT)
        return {'x': jax.random.normal(ks[0], (B, SQ, D_EMBED), jnp.float32), 'y': jax.random.normal(ks[1], (B, SKV, D_CROSS), jnp.float32), 'Wq': jax.random.normal(ks[2], (D_EMBED, D_ATT), jnp.float32) * s_e, 'bq': jax.random.normal(ks[3], (D_ATT,), jnp.float32) * 0.01, 'Wk': jax.random.normal(ks[4], (D_CROSS, D_ATT), jnp.float32) * s_c, 'bk': jax.random.normal(ks[5], (D_ATT,), jnp.float32) * 0.01, 'Wv': jax.random.normal(ks[6], (D_CROSS, D_ATT), jnp.float32) * s_c, 'bv': jax.random.normal(ks[7], (D_ATT,), jnp.float32) * 0.01, 'Wo': jax.random.normal(ks[8], (D_ATT, D_EMBED), jnp.float32) * s_a, 'bo': jax.random.normal(ks[9], (D_EMBED,), jnp.float32) * 0.01}
    _L0_xattn_all = _L0_xattn_setup()
    _L0_xattn_in = {k: v for k, v in _L0_xattn_all.items() if k in ('Wq', 'bq', 'Wk', 'bk', 'Wv', 'bv', 'Wo', 'bo')}
    del _L0_xattn_all

    def _L0_ffn_setup():
        import jax, jax.numpy as jnp
        import numpy as np
        B, S, H, E = (4, 512, 256, 8)
        key = jax.random.key(seed)
        k1, k2, k3 = jax.random.split(key, 3)
        scale_w = 1.0 / np.sqrt(H)
        return {'x': jax.random.normal(k1, (B, S, H), dtype=jnp.float32), 'router_w': jax.random.normal(k2, (H, E), dtype=jnp.float32) * scale_w, 'router_b': jnp.zeros((E,), dtype=jnp.float32), 'expert_w': jax.random.normal(k3, (E, H, H), dtype=jnp.float32) * scale_w, 'expert_b': jnp.zeros((E, H), dtype=jnp.float32)}
    _L0_ffn_all = _L0_ffn_setup()
    _L0_ffn_in = {k: v for k, v in _L0_ffn_all.items() if k in ('router_w', 'router_b', 'expert_w', 'expert_b')}
    del _L0_ffn_all
    return {'x': x, 'ctx_768': ctx_768, 'L0_xattn_Wq': _L0_xattn_in['Wq'], 'L0_xattn_bq': _L0_xattn_in['bq'], 'L0_xattn_Wk': _L0_xattn_in['Wk'], 'L0_xattn_bk': _L0_xattn_in['bk'], 'L0_xattn_Wv': _L0_xattn_in['Wv'], 'L0_xattn_bv': _L0_xattn_in['bv'], 'L0_xattn_Wo': _L0_xattn_in['Wo'], 'L0_xattn_bo': _L0_xattn_in['bo'], 'L0_ffn_router_w': _L0_ffn_in['router_w'], 'L0_ffn_router_b': _L0_ffn_in['router_b'], 'L0_ffn_expert_w': _L0_ffn_in['expert_w'], 'L0_ffn_expert_b': _L0_ffn_in['expert_b']}

def reference(x, ctx_768, L0_xattn_Wq, L0_xattn_bq, L0_xattn_Wk, L0_xattn_bk, L0_xattn_Wv, L0_xattn_bv, L0_xattn_Wo, L0_xattn_bo, L0_ffn_router_w, L0_ffn_router_b, L0_ffn_expert_w, L0_ffn_expert_b):
    import jax
    import jax.numpy as jnp

    def _L0_xattn_ref(x, y, Wq, bq, Wk, bk, Wv, bv, Wo, bo):
        import math
        import jax, jax.numpy as jnp
        import numpy as np
        B, SQ, SKV = (4, 512, 512)
        D_EMBED, D_CROSS, D_ATT, N_HEADS = (256, 192, 256, 16)
        D_HEAD = D_ATT // N_HEADS

        def _split_heads(t):
            b, s, _ = t.shape
            return t.reshape(b, s, N_HEADS, D_HEAD).transpose(0, 2, 1, 3)
        q = _split_heads(x @ Wq + bq)
        k = _split_heads(y @ Wk + bk)
        v = _split_heads(y @ Wv + bv)
        scale = 1.0 / math.sqrt(D_HEAD)
        scores = jnp.einsum('bhqd,bhkd->bhqk', q, k) * scale
        weights = jax.nn.softmax(scores, axis=-1)
        out = jnp.einsum('bhqk,bhkd->bhqd', weights, v)
        out = out.transpose(0, 2, 1, 3).reshape(x.shape[0], x.shape[1], D_ATT)
        return out @ Wo + bo

    def _L0_ffn_ref(x, router_w, router_b, expert_w, expert_b):
        import jax, jax.numpy as jnp
        import numpy as np
        B, S, H, E = (4, 512, 256, 8)
        b, s, h = x.shape
        xt = x.reshape(b * s, h)
        logits = xt @ router_w + router_b
        probs = jax.nn.softmax(logits, axis=-1)
        gate = jnp.max(probs, axis=-1)
        idx = jnp.argmax(probs, axis=-1)
        out_all = jnp.einsum('th,ehd->ted', xt, expert_w) + expert_b[None, :, :]
        e_out = jnp.take_along_axis(out_all, idx[:, None, None], axis=1)[:, 0, :]
        y = gate[:, None] * e_out
        return y.reshape(b, s, h)
    x = x + _L0_xattn_ref(_layernorm(x, axis=-1), ctx_768, L0_xattn_Wq, L0_xattn_bq, L0_xattn_Wk, L0_xattn_bk, L0_xattn_Wv, L0_xattn_bv, L0_xattn_Wo, L0_xattn_bo)
    x = x + _L0_ffn_ref(_layernorm(x, axis=-1), L0_ffn_router_w, L0_ffn_router_b, L0_ffn_expert_w, L0_ffn_expert_b)
    return x

_drawn_inputs = setup_inputs


def setup_inputs(seed=0):
    import zlib

    import numpy as np

    out = dict(_drawn_inputs(seed))
    spreads = {'L0_ffn_router_b': (0.0, 0.1), 'L0_ffn_expert_b': (0.0, 0.1)}
    factors = {'L0_xattn_bq': 7.229, 'L0_xattn_bk': 8.0, 'L0_xattn_bv': 2.707}
    for name, (base, spread) in spreads.items():
        noise = np.random.default_rng([zlib.crc32(name.encode()), seed]).standard_normal(out[name].shape)
        drawn = base * np.exp(spread * noise) if base else spread * noise
        out[name] = jnp.asarray(drawn.astype(out[name].dtype))
    for name, factor in factors.items():
        out[name] = (out[name] * factor).astype(out[name].dtype)
    return out
```

```python
from contextlib import ExitStack

import concourse.bass as bass
from concourse import mybir

ALU = mybir.AluOpType
ACT = mybir.ActivationFunctionType
F32 = mybir.dt.float32
BF16 = mybir.dt.bfloat16
AX_X = mybir.AxisListType.X

P = 128


def xattn_moe_kernel(nc, x, ctx_in, wq, bq, wk, bk, wv, bv, wo, bo, router_w, router_b, expert_w, expert_b, out):
    B, SQ, DM = x.shape
    _, SK, DC = ctx_in.shape
    NE = router_w.shape[1]
    HEADS = 16
    DH = DM // HEADS
    C = DM // P
    HC = P // DH
    T = SQ // P
    NT = B * T
    CC = 2
    DCC = DC // CC
    HB = B // 2
    EPS = 1e-5
    SCALE = DH ** -0.5
    assert DM == 256 and SQ == 256 and T == 2 and C == 2 and B % 2 == 0

    x_v = x.rearrange("b (p i) d -> b p i d", i=T)
    out_v = out.rearrange("b (p i) d -> b p i d", i=T)

    with ExitStack() as ctx:
        def sb(name, shape, dt=F32):
            return ctx.enter_context(nc.sbuf_tensor(name, shape, dt))

        def sem(name):
            return ctx.enter_context(nc.semaphore(name))

        bank = [ctx.enter_context(nc.psum_tensor(f"bank{i}", [P, 512], F32)) for i in range(2)]
        s_ps = ctx.enter_context(nc.psum_tensor("s_ps", [P, 4, 512], F32))
        pv_ps = [ctx.enter_context(nc.psum_tensor(f"pv{i}", [P, 512], F32)) for i in range(2)]

        ident = sb("ident", [P, P])
        identb = sb("identb", [P, P], BF16)
        headmask = sb("headmask", [P, HC])
        sel = sb("sel", [P, HEADS, SK], BF16)
        onespair = sb("onespair", [P, 2, 32])
        iota_e = sb("iota_e", [P, NE])
        eps_half = sb("eps_half", [P, 2])
        wq_sb = sb("wq_sb", [P, C, DM])
        wk_sb = sb("wk_sb", [DCC, CC, DM])
        wv_sb = sb("wv_sb", [DCC, CC, DM])
        wo_sb = sb("wo_sb", [P, C, DM])
        wr_sb = sb("wr_sb", [P, C, NE])
        we_sb = sb("we_sb", [P, C, NE, DM])
        bq_sb = sb("bq_sb", [P, C])
        bq_s = sb("bq_s", [P, C])
        bk_sb = sb("bk_sb", [P, C])
        bv_sb = sb("bv_sb", [SK, DM])
        bo_sb = sb("bo_sb", [P, DM])
        br_sb = sb("br_sb", [P, NE])
        be_sb = sb("be_sb", [P, NE, DM])
        ctx_sb = sb("ctx_sb", [SK, B, DC])
        ctxT = sb("ctxT", [DCC, CC, B * SK])
        kT = sb("kT", [P, C, B * SK])
        kbd = sb("kbd", [P, C, B, HC, SK])
        vpad = sb("vpad", [P, B, HEADS, 32])
        x_sb = sb("x_sb", [P, B, T, DM])
        stats = sb("stats", [P, B, T, 6])
        mv = sb("mv", [P, B, T, 2])
        rstd = sb("rstd", [P, B, T])
        xn = sb("xn", [P, 2, T, DM])
        xnT = sb("xnT", [P, 2, C, SQ])
        qT = sb("qT", [P, C, B * SQ])
        smax = sb("smax", [P, 2, T, HEADS])
        nmax = sb("nmax", [P, 2, T, 2 * HEADS], BF16)
        nmaxT = sb("nmaxT", [P, 2, SQ], BF16)
        probs = sb("probs", [P, 4, 4, SQ])
        rden = sb("rden", [P, 2, SQ])
        attnT = sb("attnT", [P, 2, C, SQ])
        stats2 = sb("stats2", [P, B, T, 6])
        mv2 = sb("mv2", [P, B, T, 2])
        rstd2 = sb("rstd2", [P, B, T])
        xn2T = sb("xn2T", [P, C, B * SQ])
        lg = sb("lg", [P, NT, NE])
        lgm = sb("lgm", [P, NT, NE])
        elg = sb("elg", [P, NT, NE])
        lmx = sb("lmx", [P, NT])
        idx = sb("idx", [P, NT])
        cand = sb("cand", [P, NT, NE])
        gate = sb("gate", [P, NT])
        ohg = sb("ohg", [P, NT, NE])

        names = ("ones ident_z const wk wv wq bkq bv ctx wo bo router we be sem_bqs "
                 "ctxT ctxT_sb kT kT_sb kbd xT xT_sb q q_sb v v_sb vpad_z probs_z nmaxT_z "
                 "bn mv rstd xn xbo "
                 "mx smax nmh nml nmT nmT_sb st exp pv rdenp attn wo_ps x2 bn2 mv2 rstd2 xn2 x2T x2T_sb "
                 "lg_ps lg rt elg ffn acc ymine out").split()
        S = {n: sem("s_" + n) for n in names}
        s_x = [sem(f"s_xload{b}") for b in range(B)]

        def jobs_of(b):
            mx = [("mx", b + 1, k) for k in range(T * HEADS // 4)] + [("nm", b + 1, 0)] if b + 1 < B else []
            done = b >= 1
            groups = [mx[0:3], mx[3:6] + [("wo", b - 1, 0)] * done, mx[6:8] + [("x2T", b - 1, 0)] * done,
                      mx[8:9] + [("lg", b - 1, 0)] * done]
            return groups

        sched = [[("mx", 0, k) for k in range(T * HEADS // 4)] + [("nm", 0, 0)]]
        for b in range(B):
            sched += jobs_of(b)
        sched.append([("wo", B - 1, 0), ("x2T", B - 1, 0), ("lg", B - 1, 0)])

        def freed_by(job):
            kind, b, k = job
            return {"mx": (S["smax"], 8 * b + k + 1), "nm": (S["nmT_sb"], b + 1), "wo": (S["x2"], b + 1),
                    "x2T": (S["x2T_sb"], b + 1), "lg": (S["lg"], b + 1)}[kind]

        flat = [j for g in sched for j in g]
        slot_of = {j: n % 2 for n, j in enumerate(flat)}
        before = {j: (flat[n - 2] if n >= 2 else None) for n, j in enumerate(flat)}

        block = ctx.enter_context(nc.Block())

        @block.sync
        def _(sp):
            for b in range(B):
                sp.dma_start(x_sb[:, b, :, :], x_v[b]).then_inc(s_x[b], 16)
                if b == 1:
                    sp.dma_start(wq_sb[:], wq.rearrange("(c p) n -> p c n", p=P)).then_inc(S["wq"], 16)
            sp.dma_start(wo_sb[:], wo.rearrange("(c p) n -> p c n", p=P)).then_inc(S["wo"], 16)
            sp.dma_start(bo_sb[:], bo.unsqueeze(0).broadcast_to([P, DM])).then_inc(S["bo"], 16)
            sp.dma_start(wr_sb[:], router_w.rearrange("(c p) n -> p c n", p=P)).then_inc(S["router"], 16)
            sp.dma_start(br_sb[:], router_b.unsqueeze(0).broadcast_to([P, NE])).then_inc(S["router"], 16)
            for c in range(C):
                sp.dma_start(we_sb[:, c], expert_w[:, c * P:(c + 1) * P, :].rearrange("e p n -> p e n")).then_inc(S["we"], 16)
            sp.dma_start(be_sb[:].rearrange("p e n -> p (e n)"),
                         expert_b.rearrange("e n -> (e n)").unsqueeze(0).broadcast_to([P, NE * DM])).then_inc(S["be"], 16)
            for t in range(NT):
                sp.wait_ge(S["acc"], (2 * NE + 0) * (t + 1))
                if t % T == T - 1:
                    sp.dma_start(out_v[t // T], x_sb[:, t // T, :, :]).then_inc(S["out"], 16)
            sp.wait_ge(S["out"], 16 * B)

        @block.gpsimd
        def _(pool):
            g = nc.gpsimd
            g.memset(ident[:], 0.0).then_inc(S["ident_z"], 1)
            g.memset(identb[:], 0.0).then_inc(S["ident_z"], 1)
            g.memset(sel[:], 0.0).then_inc(S["ident_z"], 1)
            g.memset(headmask[:], 1.0).then_inc(S["ident_z"], 1)
            g.memset(onespair[:], 0.0).then_inc(S["ident_z"], 1)
            g.memset(eps_half[:], -0.5).then_inc(S["ident_z"], 1)
            g.iota(iota_e[:], pattern=[[1, NE]], base=0, channel_multiplier=0,
                   allow_small_or_imprecise_dtypes=True).then_inc(S["ident_z"], 1)
            pool.wait_ge(S["ident_z"], 7)
            for m in (ident, identb):
                g.affine_select(out=m[:], in_=m[:], compare_op=ALU.not_equal, fill=1.0, base=0,
                                pattern=[[-1, P]], channel_multiplier=1).then_inc(S["const"], 1)
            for par in range(2):
                g.memset(onespair[:, par, 16 * par:16 * par + 16], 1.0).then_inc(S["const"], 1)
            g.memset(vpad[:], 0.0).then_inc(S["vpad_z"], 1)
            g.affine_select(out=headmask[:], in_=headmask[:], compare_op=ALU.is_ge, fill=0.0, base=0,
                            pattern=[[-DH, HC]], channel_multiplier=1).then_inc(S["const"], 1)
            pool.wait_ge(S["const"], 5)
            g.affine_select(out=headmask[:], in_=headmask[:], compare_op=ALU.is_ge, fill=0.0, base=DH - 1,
                            pattern=[[DH, HC]], channel_multiplier=-1).then_inc(S["const"], 1)
            for half in range(2):
                pool.wait_ge(S["const"], 6 + half)
                g.affine_select(out=sel[:], in_=sel[:], compare_op=ALU.not_equal, fill=1.0, base=-HEADS * half,
                                pattern=[[-1, HEADS], [0, SK]], channel_multiplier=1).then_inc(S["const"], 1)
            g.memset(nmaxT[:], 0.0).then_inc(S["nmaxT_z"], 1)

            def inv_std(b, mv_, rstd_, ready, done):
                pool.wait_ge(S[ready], b + 1)
                g.tensor_tensor(rstd_[:, b, :], mv_[:, b, :, 1], eps_half[:, 0:T], ALU.pow).then_inc(S[done], 1)

            pool.wait_ge(S["const"], 8)
            for b in range(B):
                inv_std(b, mv, rstd, "mv", "rstd")
                pool.wait_ge(S["kT_sb"], 2 * (b // HB + 1))
                for c in range(C):
                    k_b = kT[:, c, b * SK:(b + 1) * SK]
                    g.tensor_tensor(kbd[:, c, b], k_b.unsqueeze(1).broadcast_to([P, HC, SK]),
                                    headmask[:].unsqueeze(2).broadcast_to([P, HC, SK]), ALU.mult).then_inc(S["kbd"], 1)
            for b in range(B):
                pool.wait_ge(S["xn"], T * (b + 1))
                if b == 0:
                    pool.wait_ge(S["bo"], 16)
                g.tensor_tensor(x_sb[:, b], x_sb[:, b], bo_sb[:].unsqueeze(1).broadcast_to([P, T, DM]),
                                ALU.add).then_inc(S["xbo"], 1)
            for b in range(B):
                inv_std(b, mv2, rstd2, "mv2", "rstd2")

        @block.scalar
        def _(act):
            a = nc.scalar
            act.dma_start(ctx_sb[:], ctx_in.rearrange("b s d -> s b d")).then_inc(S["ctx"], 16)
            act.dma_start(wk_sb[:], wk.rearrange("(c p) n -> p c n", p=DCC)).then_inc(S["wk"], 16)
            act.dma_start(bk_sb[:], bk.rearrange("(c p) -> p c", p=P), allow_slow_non_contiguous=True).then_inc(S["bkq"], 16)
            act.dma_start(bq_sb[:], bq.rearrange("(c p) -> p c", p=P), allow_slow_non_contiguous=True).then_inc(S["bkq"], 16)
            act.dma_start(wv_sb[:], wv.rearrange("(c p) n -> p c n", p=DCC)).then_inc(S["wv"], 16)
            act.dma_start(bv_sb[:], bv.unsqueeze(0).broadcast_to([SK, DM])).then_inc(S["bv"], 16)
            act.wait_ge(S["bkq"], 32)
            a.mul(bq_s[:], bq_sb[:], SCALE).then_inc(S["sem_bqs"], 1)
            act.wait_ge(S["sem_bqs"], 1)
            for n in range(4):
                c, half = n // 2, n % 2
                act.wait_ge(S["ctxT"], n + 1)
                a.copy(ctxT[:, c, half * HB * SK:(half + 1) * HB * SK],
                       s_ps[0:DCC, n, 0:HB * SK]).then_inc(S["ctxT_sb"], 1)
            kbanks = [bank[0], bank[1], pv_ps[0], pv_ps[1]]
            for n in range(4):
                half, m = n // 2, n % 2
                act.wait_ge(S["kT"], n + 1)
                a.activation(kT[:, m, half * HB * SK:(half + 1) * HB * SK], kbanks[n][:, 0:HB * SK], ACT.Identity,
                             bias=bk_sb[:, m:m + 1]).then_inc(S["kT_sb"], 1)
            for b in range(B):
                act.wait_ge(S["xT"], b + 1)
                if b >= 2:
                    act.wait_ge(S["q"], b - 1)
                a.copy(xnT[:, b % 2].rearrange("p c s -> p (c s)"), bank[b % 2][:]).then_inc(S["xT_sb"], 1)
                act.wait_ge(S["q"], b + 1)
                for m in range(C):
                    a.activation(qT[:, m, b * SQ:(b + 1) * SQ], s_ps[:, b % 2, m * SQ:(m + 1) * SQ], ACT.Identity,
                                 bias=bq_s[:, m:m + 1], scale=SCALE).then_inc(S["q_sb"], 1)

            def copy_nmaxT(b):
                act.wait_ge(S["nmT"], b + 1)
                if b == 0:
                    act.wait_ge(S["nmaxT_z"], 1)
                if b >= 2:
                    act.wait_ge(S["st"], 4 * (b - 1))
                src = bank[slot_of[("nm", b, 0)]][0:2 * HEADS, 0:P].bitcast(BF16)
                a.copy(nmaxT[0:2 * HEADS, b % 2, :], src).then_inc(S["nmT_sb"], 1)

            def copy_x2T(b):
                act.wait_ge(S["x2T"], b + 1)
                a.copy(xn2T[:, :, b * SQ:(b + 1) * SQ],
                       bank[slot_of[("x2T", b, 0)]][:].rearrange("p (c s) -> p c s", c=C)).then_inc(S["x2T_sb"], 1)

            copy_nmaxT(0)
            act.wait_ge(S["probs_z"], 1)
            for b in range(B):
                for q in range(4):
                    n = 4 * b + q
                    act.wait_ge(S["st"], n + 1)
                    if n >= 4:
                        act.wait_ge(S["pv"], (n - 4) // 2 + 1)
                    a.activation(probs[0:SK, n % 4].rearrange("p (a j) s -> p a (j s)", a=2),
                                 s_ps[0:SK, 2 * (n % 2):2 * (n % 2) + 2, :], ACT.Exp).then_inc(S["exp"], 1)
                    if q == 2 and b >= 1:
                        copy_x2T(b - 1)
                if b + 1 < B:
                    copy_nmaxT(b + 1)
            copy_x2T(B - 1)
            act.wait_ge(S["rt"], 2)
            a.activation(elg[:], lgm[:], ACT.Exp).then_inc(S["elg"], 1)

        @block.vector
        def _(dve):
            v = nc.vector

            def layer_norm(b, src, stats_, mv_, rstd_, names_, first):
                bn_, mv_n, rstd_n, xn_n = names_
                for i in range(T):
                    v.bn_stats(stats_[:, b, i, :], src[:, b, i, :]).then_inc(S[bn_], 1)
                for i in range(T):
                    dve.wait_ge(S[bn_], T * b + i + 1)
                    last = v.bn_aggr(mv_[:, b, i, :], stats_[:, b, i, :])
                    last.then_inc(S[bn_ + "a"], 1)
                dve.wait_ge(S[bn_ + "a"], T * (b + 1))
                v.tensor_scalar(mv_[:, b, :, 1], mv_[:, b, :, 1], EPS, None, ALU.add).then_inc(S[mv_n], 1)

            def normalise(b, src, mv_, rstd_, rstd_n, xn_n):
                dve.wait_ge(S[rstd_n], b + 1)
                for i in range(T):
                    v.tensor_scalar(xn[:, b % 2, i, :], src[:, b, i, :], mv_[:, b, i, 0:1], rstd_[:, b, i:i + 1],
                                    ALU.subtract, ALU.mult).then_inc(S[xn_n], 1)

            v.memset(probs[64:P], 0.0).then_inc(S["probs_z"], 1)
            S["bna"], S["bn2a"] = sem("s_bna"), sem("s_bn2a")
            for b in range(B + 1):
                if b < B:
                    dve.wait_ge(s_x[b], 16)
                    layer_norm(b, x_sb, stats, mv, rstd, ("bn", "mv", "rstd", "xn"), True)
                if b >= 1:
                    if b - 1 == 0:
                        dve.wait_ge(S["vpad_z"], 1)
                        dve.wait_ge(S["bv"], 16)
                    else:
                        pass
                if b < B:
                    if b >= 2:
                        dve.wait_ge(S["xT"], b - 1)
                    normalise(b, x_sb, mv, rstd, "rstd", "xn")
                if b >= 1:
                    n = b - 1
                    dve.wait_ge(S["v"], n + 1)
                    for par in range(2):
                        v.tensor_tensor(
                            vpad[0:SK, n].rearrange("p (j r) e -> p j r e", r=2)[:, :, par, 16 * par:16 * par + 16],
                            s_ps[0:SK, 2 + n % 2, 0:DM].rearrange("p (j r e) -> p j r e", r=2, e=DH)[:, :, par, :],
                            bv_sb[:].rearrange("p (j r e) -> p j r e", r=2, e=DH)[:, :, par, :],
                            ALU.add).then_inc(S["v_sb"], 1)

            def max_jobs(b, ks):
                for k in ks:
                    i, grp = k // 4, k % 4
                    dve.wait_ge(S["mx"], 8 * b + k + 1)
                    if b >= 2 and k == 0:
                        dve.wait_ge(S["nml"], b - 1)
                    v.tensor_reduce(smax[:, b % 2, i, 4 * grp:4 * grp + 4],
                                    bank[slot_of[("mx", b, k)]][:, 0:4 * SK].rearrange("p (h k) -> p h k", k=SK),
                                    AX_X, ALU.max).then_inc(S["smax"], 1)

            def neg_max(b):
                dve.wait_ge(S["smax"], 8 * (b + 1))
                if b >= 2:
                    dve.wait_ge(S["nmT"], b - 1)
                v.tensor_scalar(nmax[:, b % 2, :, 0:HEADS], smax[:, b % 2], -1.0, None, ALU.mult).then_inc(S["nmh"], 1)
                dve.wait_ge(S["nmh"], b + 1)
                v.scalar_tensor_tensor(out=nmax[:, b % 2, :, HEADS:2 * HEADS], in0=smax[:, b % 2], scalar=-1.0,
                                       in1=nmax[:, b % 2, :, 0:HEADS], op0=ALU.mult, op1=ALU.subtract).then_inc(S["nml"], 1)

            def divide(b, c):
                n = 2 * b + c
                dve.wait_ge(S["pv"], n + 1)
                if n >= 1:
                    dve.wait_ge(S["attn"], n)
                v.reciprocal(rden[:, c], pv_ps[c][:, SQ:2 * SQ]).then_inc(S["rdenp"], 1)
                dve.wait_ge(S["rdenp"], n + 1)
                if b >= 2:
                    dve.wait_ge(S["wo_ps"], b - 1)
                v.tensor_tensor(attnT[:, b % 2, c], pv_ps[c][:, 0:SQ], rden[:, c], ALU.mult).then_inc(S["attn"], 1)

            def residual(b):
                dve.wait_ge(S["wo_ps"], b + 1)
                dve.wait_ge(S["xbo"], b + 1)
                v.tensor_tensor(x_sb[:, b], bank[slot_of[("wo", b, 0)]][:].rearrange("p (i d) -> p i d", i=T),
                                x_sb[:, b], ALU.add).then_inc(S["x2"], 1)
                dve.wait_ge(S["x2"], b + 1)
                layer_norm(b, x_sb, stats2, mv2, rstd2, ("bn2", "mv2", "rstd2", "xn2"), False)

            def norm2(b):
                if b >= 2:
                    dve.wait_ge(S["x2T"], b - 1)
                normalise(b, x_sb, mv2, rstd2, "rstd2", "xn2")

            def logits(b):
                dve.wait_ge(S["lg_ps"], b + 1)
                v.tensor_tensor(lg[:, T * b:T * b + T],
                                bank[slot_of[("lg", b, 0)]][:, 0:T * NE].rearrange("p (i e) -> p i e", i=T),
                                br_sb[:].unsqueeze(1).broadcast_to([P, T, NE]), ALU.add).then_inc(S["lg"], 1)

            max_jobs(0, range(8))
            neg_max(0)
            dve.wait_ge(S["router"], 32)
            for b in range(B):
                if b >= 1:
                    divide(b - 1, 1)
                if b + 1 < B:
                    max_jobs(b + 1, range(0, 6))
                if b >= 1:
                    residual(b - 1)
                if b + 1 < B:
                    max_jobs(b + 1, range(6, 8))
                    neg_max(b + 1)
                if b >= 1:
                    norm2(b - 1)
                divide(b, 0)
                if b >= 1:
                    logits(b - 1)
            divide(B - 1, 1)
            residual(B - 1)
            norm2(B - 1)
            logits(B - 1)

            dve.wait_ge(S["lg"], B)
            v.tensor_reduce(lmx[:], lg[:], AX_X, ALU.max).then_inc(S["rt"], 1)
            dve.wait_ge(S["rt"], 1)
            v.tensor_tensor(lgm[:], lg[:], lmx[:].unsqueeze(2).broadcast_to([P, NT, NE]), ALU.subtract).then_inc(S["rt"], 1)
            dve.wait_ge(S["rt"], 2)
            v.tensor_scalar(cand[:], lgm[:], 0.0, float(NE), ALU.is_lt, ALU.mult).then_inc(S["rt"], 1)
            dve.wait_ge(S["rt"], 3)
            v.tensor_tensor(cand[:], cand[:], iota_e[:].unsqueeze(1).broadcast_to([P, NT, NE]), ALU.add).then_inc(S["rt"], 1)
            dve.wait_ge(S["rt"], 4)
            v.tensor_reduce(idx[:], cand[:], AX_X, ALU.min).then_inc(S["rt"], 1)
            dve.wait_ge(S["rt"], 5)
            v.tensor_tensor(ohg[:], cand[:], idx[:].unsqueeze(2).broadcast_to([P, NT, NE]), ALU.is_equal).then_inc(S["rt"], 1)
            dve.wait_ge(S["elg"], 1)
            v.tensor_reduce(gate[:], elg[:], AX_X, ALU.add).then_inc(S["rt"], 1)
            dve.wait_ge(S["rt"], 7)
            v.reciprocal(gate[:], gate[:]).then_inc(S["rt"], 1)
            dve.wait_ge(S["rt"], 8)
            v.tensor_tensor(ohg[:], ohg[:], gate[:].unsqueeze(2).broadcast_to([P, NT, NE]), ALU.mult).then_inc(S["rt"], 1)
            dve.wait_ge(S["rt"], 9)
            dve.wait_ge(S["be"], 16)
            n = 0
            for t in range(NT):
                y = x_sb[:, t // T, t % T, :]
                for e in range(NE):
                    if n:
                        dve.wait_ge(S["acc"], n)
                    v.scalar_tensor_tensor(out=y, in0=be_sb[:, e, :], scalar=ohg[:, t, e:e + 1], in1=y,
                                           op0=ALU.mult, op1=ALU.add).then_inc(S["acc"], 1)
                    n += 1
                    g = (NE // 2) * t + e // 2
                    dve.wait_ge(S["ffn"], g + 1)
                    dve.wait_ge(S["acc"], n)
                    v.scalar_tensor_tensor(out=y, in0=s_ps[:, g % 4, (e % 2) * DM:(e % 2 + 1) * DM],
                                           scalar=ohg[:, t, e:e + 1], in1=y,
                                           op0=ALU.mult, op1=ALU.add).then_inc(S["acc"], 1)
                    n += 1

        @block.tensor
        def _(pe):
            m_ = nc.tensor.matmul
            pe.wait_ge(S["const"], 8)
            pe.wait_ge(S["ctx"], 16)
            for n in range(4):
                c, half = n // 2, n % 2
                for b in range(HB):
                    last = nc.tensor.transpose(s_ps[0:DCC, n, b * SK:(b + 1) * SK],
                                               ctx_sb[:, half * HB + b, c * DCC:(c + 1) * DCC], ident[0:SK, 0:SK])
                last.then_inc(S["ctxT"], 1)
            kbanks = [bank[0], bank[1], pv_ps[0], pv_ps[1]]
            pe.wait_ge(S["wk"], 16)
            for n in range(4):
                half, m = n // 2, n % 2
                pe.wait_ge(S["ctxT_sb"], half + 3)
                for c in range(CC):
                    last = m_(kbanks[n][:, 0:HB * SK], wk_sb[:, c, m * P:(m + 1) * P],
                              ctxT[:, c, half * HB * SK:(half + 1) * HB * SK], start=(c == 0), stop=(c == CC - 1))
                last.then_inc(S["kT"], 1)
            pe.wait_ge(S["wv"], 16)
            pe.wait_ge(S["wq"], 16)
            pe.wait_ge(S["ctxT_sb"], 4)

            def values(b):
                if b >= 2:
                    pe.wait_ge(S["v_sb"], 2 * (b - 1))
                for c in range(CC):
                    last = m_(s_ps[0:SK, 2 + b % 2, 0:DM], ctxT[:, c, b * SK:(b + 1) * SK], wv_sb[:, c, :],
                              start=(c == 0), stop=(c == CC - 1))
                last.then_inc(S["v"], 1)

            def x_transposes(b):
                pe.wait_ge(S["xn"], T * (b + 1))
                if b >= 2:
                    pe.wait_ge(S["xT_sb"], b - 1)
                else:
                    pe.wait_ge(S["kT_sb"], b + 1)
                for c in range(C):
                    for i in range(T):
                        last = nc.tensor.transpose(bank[b % 2][:, c * SQ + i * P:c * SQ + (i + 1) * P],
                                                   xn[:, b % 2, i, c * P:(c + 1) * P], ident[:])
                last.then_inc(S["xT"], 1)

            def queries(b):
                pe.wait_ge(S["xT_sb"], b + 1)
                if b >= 2:
                    pe.wait_ge(S["q_sb"], 2 * (b - 1))
                for m in range(C):
                    for c in range(C):
                        last = m_(s_ps[:, b % 2, m * SQ:(m + 1) * SQ], wq_sb[:, c, m * P:(m + 1) * P],
                                  xnT[:, b % 2, c, :], start=(c == 0), stop=(c == C - 1))
                last.then_inc(S["q"], 1)

            for b in range(B):
                x_transposes(b)
                values(b)
                queries(b)

            def job(j):
                kind, b, k = j
                dst = bank[slot_of[j]]
                if before[j] is not None:
                    pe.wait_ge(*freed_by(before[j]))
                if kind == "mx":
                    i, grp = k // 4, k % 4
                    c, h0 = grp // 2, 4 * (grp % 2)
                    pe.wait_ge(S["kbd"], 2 * b + c + 1)
                    m_(dst[:, 0:4 * SK], qT[:, c, b * SQ + i * P:b * SQ + (i + 1) * P],
                       kbd[:, c, b, h0:h0 + 4, :].rearrange("p h k -> p (h k)"), start=True, stop=True).then_inc(S["mx"], 1)
                elif kind == "nm":
                    pe.wait_ge(S["nml"], b + 1)
                    d = dst[0:2 * HEADS, 0:P].bitcast(BF16)
                    for i in range(T):
                        last = nc.tensor.transpose(d[:, i * P:(i + 1) * P], nmax[:, b % 2, i, :], identb[:])
                    last.then_inc(S["nmT"], 1)
                elif kind == "wo":
                    pe.wait_ge(S["attn"], 2 * (b + 1))
                    for i in range(T):
                        for c in range(C):
                            last = m_(dst[:, i * DM:(i + 1) * DM], attnT[:, b % 2, c, i * P:(i + 1) * P], wo_sb[:, c, :],
                                      start=(c == 0), stop=(c == C - 1))
                    last.then_inc(S["wo_ps"], 1)
                elif kind == "x2T":
                    pe.wait_ge(S["xn2"], T * (b + 1))
                    for c in range(C):
                        for i in range(T):
                            last = nc.tensor.transpose(dst[:, c * SQ + i * P:c * SQ + (i + 1) * P],
                                                       xn[:, b % 2, i, c * P:(c + 1) * P], ident[:])
                    last.then_inc(S["x2T"], 1)
                else:
                    pe.wait_ge(S["x2T_sb"], b + 1)
                    for i in range(T):
                        for c in range(C):
                            last = m_(dst[:, i * NE:(i + 1) * NE], xn2T[:, c, b * SQ + i * P:b * SQ + (i + 1) * P],
                                      wr_sb[:, c, :], start=(c == 0), stop=(c == C - 1))
                    last.then_inc(S["lg_ps"], 1)

            def scores(n):
                b, c, par = n // 4, n % 4 // 2, n % 2
                if n >= 2:
                    pe.wait_ge(S["exp"], n - 1)
                for j in range(4):
                    hl = 2 * j + par
                    dst = s_ps[0:SK, 2 * (n % 2) + j // 2, (j % 2) * SQ:(j % 2 + 1) * SQ]
                    m_(dst, kbd[:, c, b, hl, :], qT[:, c, b * SQ:(b + 1) * SQ], start=True, stop=False)
                    last = m_(dst, sel[:, HC * c + hl, :], nmaxT[:, b % 2, :], start=False, stop=True)
                last.then_inc(S["st"], 1)

            def weighted(n):
                b, c, par = n // 4, n % 4 // 2, n % 2
                pe.wait_ge(S["exp"], n + 1)
                if par == 0 and b >= 1:
                    pe.wait_ge(S["attn"], 2 * (b - 1) + c + 1)
                for j in range(4):
                    m_(pv_ps[c][32 * j:32 * j + 32, 0:SQ], vpad[:, b, HC * c + 2 * j + par, :], probs[:, n % 4, j, :],
                       start=(par == 0), stop=(par == 1))
                if par == 1:
                    for r in range(2):
                        for j in range(4):
                            last = m_(pv_ps[c][32 * j:32 * j + 32, SQ:2 * SQ], onespair[:, r, :],
                                      probs[:, (n - 1 + r) % 4, j, :], start=(r == 0), stop=(r == 1))
                    last.then_inc(S["pv"], 1)

            pe.wait_ge(S["q_sb"], 2 * B)
            pe.wait_ge(S["v_sb"], 2 * B)
            for j in sched[0]:
                job(j)
            pe.wait_ge(S["wo"], 16)
            pe.wait_ge(S["router"], 32)
            for n in range(4 * B):
                b = n // 4
                if n % 4 == 0:
                    pe.wait_ge(S["nmT_sb"], b + 1)
                scores(n)
                if n >= 1:
                    weighted(n - 1)
                for j in sched[1 + n]:
                    job(j)
            weighted(4 * B - 1)
            for j in sched[-1]:
                job(j)

            pe.wait_ge(S["we"], 16 * C)
            pe.wait_ge(S["exp"], 4 * B)
            for t in range(NT):
                for e2 in range(NE // 2):
                    g = (NE // 2) * t + e2
                    if g >= 4:
                        pe.wait_ge(S["acc"], 4 * (g - 4) + 4)
                    for c in range(C):
                        last = m_(s_ps[:, g % 4, :], xn2T[:, c, t * P:(t + 1) * P],
                                  we_sb[:, c, 2 * e2:2 * e2 + 2, :].rearrange("p e n -> p (e n)"),
                                  start=(c == 0), stop=(c == C - 1))
                    last.then_inc(S["ffn"], 1)


_INS = ['x', 'ctx_768', 'L0_xattn_Wq', 'L0_xattn_bq', 'L0_xattn_Wk', 'L0_xattn_bk', 'L0_xattn_Wv', 'L0_xattn_bv',
        'L0_xattn_Wo', 'L0_xattn_bo', 'L0_ffn_router_w', 'L0_ffn_router_b', 'L0_ffn_expert_w', 'L0_ffn_expert_b']
_OUTS = [((8, 256, 256), 'float32')]


def kernel(**inputs):
    import numpy as _np
    import concourse.bacc as _bacc
    from concourse import mybir as _mybir
    from concourse.bass_utils import run_bass_kernel_spmd as _run

    nc = _bacc.Bacc("TRN2", target_bir_lowering=False, num_devices=1)
    arrays, args = {}, []
    for name in _INS:
        a = _np.ascontiguousarray(inputs[name])
        arrays[f"in_{name}_dram"] = a
        args.append(nc.dram_tensor(f"in_{name}_dram", a.shape, _mybir.dt.from_np(a.dtype), kind="ExternalInput").ap())
    for i, (shape, dtype) in enumerate(_OUTS):
        dt = _mybir.dt.from_np(_np.dtype(dtype))
        args.append(nc.dram_tensor(f"out_{i}_dram", shape, dt, kind="ExternalOutput").ap())
    xattn_moe_kernel(nc, *args)
    r = _run(nc, [arrays], core_ids=[0])
    got = tuple(r.results[0][f"out_{i}_dram"] for i in range(len(_OUTS)))
    return got[0]
```

```python
from contextlib import ExitStack

import numpy as np

import concourse.bass as bass
from concourse import mybir

ALU = mybir.AluOpType
ACT = mybir.ActivationFunctionType
F32 = mybir.dt.float32
BF16 = mybir.dt.bfloat16
I32 = mybir.dt.int32
U32 = mybir.dt.uint32
AX_X = mybir.AxisListType.X

P = 128
TWO_BF16_ONES = float(np.array([0x3F803F80], np.uint32).view(np.float32)[0])


def xattn_moe_kernel(nc, x, ctx_in, wq, bq, wk, bk, wv, bv, wo, bo, router_w, router_b, expert_w, expert_b, out):
    B, SQ, DM = x.shape
    _, SK, DC = ctx_in.shape
    NE = router_w.shape[1]
    HEADS = 16
    DH = DM // HEADS
    C = DM // P
    HC = P // DH
    T = SQ // P
    NT = B * T
    CC = 2
    DCC = DC // CC
    U = HEADS // 2
    HB = B // 2
    EPS = 1e-5
    QBLK, KBLK = (0, 0, 0, 1, 1, 2), (0, 1, 2, 0, 1, 0)
    NBLK = len(QBLK)
    QRING = 4
    SCALE = DH ** -0.5
    RB = B - 2
    RT = RB * T
    ST = RT + NE - 1
    XRING, YRING = 6, 4
    assert DM == 256 and SQ == 256 and T == 2 and C == 2 and B % 2 == 0

    x_v = x.rearrange("b (p i) d -> b p i d", i=T)
    out_v = out.rearrange("b (p i) d -> b p i d", i=T)

    q_dram = nc.dram_tensor("q_parts", (B, 3, DM, SQ), BF16, kind="Internal").ap()
    sorted_x = nc.dram_tensor("sorted_x", (ST * P, DM), F32, kind="Internal").ap()
    sorted_y = nc.dram_tensor("sorted_y", (ST * P, DM), F32, kind="Internal").ap()
    k_dram = nc.dram_tensor("k_parts", (3, DM, B * SK), BF16, kind="Internal").ap()

    with ExitStack() as ctx:
        def sb(name, shape, dt=F32):
            return ctx.enter_context(nc.sbuf_tensor(name, shape, dt))

        def sem(name):
            return ctx.enter_context(nc.semaphore(name))

        NBANK = 4
        bank = [ctx.enter_context(nc.psum_tensor(f"bank{i}", [P, 512], F32)) for i in range(NBANK)]
        s_ps = [ctx.enter_context(nc.psum_tensor(f"s_ps{i}", [P, 512], F32)) for i in range(2)]
        pv_ps = [ctx.enter_context(nc.psum_tensor(f"pv_ps{i}", [P, 512], F32)) for i in range(2)]

        ident = sb("ident", [P, P])
        identb = sb("identb", [P, P], BF16)
        iota_e = sb("iota_e", [P, NE])
        minus_half = sb("minus_half", [P, T])
        before_me = sb("before_me", [P, P], BF16)
        all_ones = sb("all_ones", [P, P], BF16)
        upto = sb("upto", [P, NE, NE])
        iota_t = sb("iota_t", [P, ST])
        iota_rows = sb("iota_rows", [P, RT])
        wq_sb = sb("wq_sb", [P, C, DM])
        wk_sb = sb("wk_sb", [DCC, CC, DM])
        wv_sb = sb("wv_sb", [DCC, CC, DM])
        wo_sb = sb("wo_sb", [P, C, DM])
        wr_sb = sb("wr_sb", [P, C, NE])
        we_sb = sb("we_sb", [P, C, NE, DM])
        bq_sb = sb("bq_sb", [P, C])
        bq_s = sb("bq_s", [P, C])
        bk_sb = sb("bk_sb", [P, C])
        bv_sb = sb("bv_sb", [P, C])
        bv_bc = sb("bv_bc", [P, C, P])
        bo_sb = sb("bo_sb", [P, DM])
        br_sb = sb("br_sb", [P, NE])
        be_sb = sb("be_sb", [P, NE, DM])
        ctx_sb = sb("ctx_sb", [SK, B, DC])
        ctxT = sb("ctxT", [DCC, CC, B * SK])
        KROWS = NBLK * DH + 2
        kT = sb("kT", [P, C, B * SK])
        kr = sb("kr", [P, C, B * SK])
        kpart = sb("kpart", [P, 3, C, B * SK], BF16)
        kst = sb("kst", [KROWS, HEADS, B * SK], BF16)
        q32 = sb("q32", [P, C, SQ])
        qr = sb("qr", [P, C, SQ])
        qpart = sb("qpart", [P, 2, 3, C, SQ], BF16)
        qst = sb("qst", [KROWS, QRING, HEADS, SQ], BF16)
        vaug = sb("vaug", [P, B, HEADS, 32])
        x_sb = sb("x_sb", [P, B, T, DM])
        stats = sb("stats", [P, B, T, 6])
        mv = sb("mv", [P, B, T, 2])
        rstd = sb("rstd", [P, B, T])
        xn = sb("xn", [P, T, DM])
        xnT = sb("xnT", [P, C, SQ])
        smax = sb("smax", [P, T, HEADS])
        nmax = sb("nmax", [P, T, 2 * HEADS], BF16)
        nmaxT = sb("nmaxT", [2 * HEADS, SQ], BF16)
        probs = sb("probs", [P, 4, 2, SQ])
        rawT = sb("rawT", [P, 4, SQ])
        rden = sb("rden", [P, T, HEADS])
        attn = sb("attn", [P, T, DM])
        attnT = sb("attnT", [P, C, SQ])
        stats2 = sb("stats2", [P, B, T, 6])
        mv2 = sb("mv2", [P, B, T, 2])
        rstd2 = sb("rstd2", [P, B, T])
        xn2 = sb("xn2", [P, B, T, DM])
        xn2T = sb("xn2T", [P, C, 2, SQ])
        lg = sb("lg", [P, NT, NE])
        lgm = sb("lgm", [P, NT, NE])
        elg = sb("elg", [P, NT, NE])
        lmx = sb("lmx", [P, NT])
        idx = sb("idx", [P, NT])
        cand = sb("cand", [P, NT, NE])
        gate = sb("gate", [P, NT])
        ohg = sb("ohg", [P, NT, NE])
        oh = sb("oh", [P, RT + 1, NE], BF16)
        over = sb("over", [P, NE, RT])
        tiles_of = sb("tiles_of", [P, NE])
        prefix = sb("prefix", [P, NE, NE])
        end_tile = sb("end_tile", [P, NE])
        start_tile = sb("start_tile", [P, NE])
        row_e = sb("row_e", [P, RT, NE])
        row_f = sb("row_f", [P, RT])
        row = sb("row", [P, RT], I32)
        past = sb("past", [1, ST, NE])
        exp_f = sb("exp_f", [1, ST])
        exp_of = sb("exp_of", [1, ST], I32)
        zeros = kr[:, 0, 0:DM]
        xs = [kpart[:].rearrange("p t c k -> p (t c k)").bitcast(F32)[:, n * DM:(n + 1) * DM] for n in range(XRING)]
        ys = [kT[:].rearrange("p c k -> p (c k)")[:, n * DM:(n + 1) * DM] for n in range(YRING)]
        xsT = [qr[:, n] for n in range(2)]

        names = ("zeroed ident sel vaug_z vaug_set kst_ones probs_z wq wk wv bcol ctx wo bo router we be bqs bvb "
                 "ctxT ctxT_sb kT kT_sb kh kr km kl kwr krd xT xT_sb q q_sb qh qr qm ql nmrow "
                 "v v_sb bn1 ag1 var1 rstd1 xn1 bvo bo2 xbias mx smax nmh nml nm nm_sb "
                 "scores exp pv pv_sb oT rec onorm aT aT_sb wo_ps x2 bn2 ag2 var2 rstd2 xn2 x2T x2T_sb "
                 "lg_ps lg rt elg ffn acc out "
                 "sort_c oh_z zeros zfill rank sortd st exp_of scattered xsT xsT_sb y y_sb gated comb").split()
        S = {n: sem("s_" + n) for n in names}
        s_qwr = [sem(f"s_qwr{i}") for i in range(2)]
        s_qrd = [sem(f"s_qrd{i}") for i in range(QRING)]
        s_xs = [sem(f"s_xs{i}") for i in range(XRING)]
        s_ys = [sem(f"s_ys{i}") for i in range(YRING)]
        s_back = [sem(f"s_back{b}") for b in range(RB)]
        s_xload = [sem(f"s_xload{b}") for b in range(B)]

        FRONT, MAXI, BACK = 3, 1, -1
        STEPS = range(-FRONT, B + 2)

        def valid(b):
            return 0 <= b < B

        def jobs_at(step, u):
            m, f, k = step + MAXI, step + FRONT, step + BACK
            plan = {
                0: [("x2T", k - 1, 0)] * (step < B) + [("mx", m, 0), ("mx", m, 1), ("mx", m, 2)],
                1: [("mx", m, 3), ("mx", m, 4)],
                2: [("oT", k, 0), ("oT", k, 1)] + [("lg", k - 1, 0)] * (step < B),
                3: [("mx", m, 5), ("mx", m, 6), ("mx", m, 7)],
                4: [("aT", k, 0), ("v", f, 0)] + [("rank", 0, 0)] * (step == RB + 1),
                5: [("nm", m, 0), ("wo", k, 0)],
                6: [("xT", f, 0)] + ([("bvo", step + 2, 0)] if step == -2 else []),
                7: [("q", f, 0)],
            }[u]
            plan = plan + {(B, 7): [("x2T", B - 2, 0)], (B + 1, 0): [("lg", B - 2, 0)], (B + 1, 1): [("x2T", B - 1, 0)],
                     (B + 1, 3): [("lg", B - 1, 0)]}.get((step, u), [])
            return [j for j in plan if valid(j[1])]

        def sorted_at(step, u):
            if step < B:
                return range(0)
            first = {B: (0, 0, 0, 0, 1, 2, 4, 6, 9), B + 1: (9, 11, 13, 15, 17, ST, ST, ST, ST)}[step]
            return range(first[u], first[u + 1])

        order = [j for step in STEPS for u in range(U) for j in jobs_at(step, u)]
        bank_of = {j: bank[n % NBANK] for n, j in enumerate(order)}
        before = {j: (order[n - NBANK] if n >= NBANK else None) for n, j in enumerate(order)}

        def freed_by(job):
            kind, b, k = job
            return {"mx": (S["smax"], 8 * b + k + 1), "nm": (S["nm_sb"], b + 1), "wo": (S["x2"], b + 1),
                    "x2T": (S["x2T_sb"], b + 1), "lg": (S["lg"], b + 1), "oT": (S["onorm"], T * b + k + 1),
                    "aT": (S["aT_sb"], b + 1), "xT": (S["xT_sb"], b + 1), "q": (S["q_sb"], C * (b + 1)),
                    "v": (S["v_sb"], b + 1), "rank": (S["sortd"], 5),
                    "bvo": (S["bo2"], 1)}[kind]

        block = ctx.enter_context(nc.Block())

        @block.sync
        def _(sp):
            sp.dma_start(x_sb[:, 0], x_v[0]).then_inc(s_xload[0], 16)
            sp.dma_start(wq_sb[:], wq.rearrange("(c p) n -> p c n", p=P)).then_inc(S["wq"], 16)
            for b in range(1, 4):
                sp.dma_start(x_sb[:, b], x_v[b]).then_inc(s_xload[b], 16)
            sp.dma_start(wo_sb[:], wo.rearrange("(c p) n -> p c n", p=P)).then_inc(S["wo"], 16)
            sp.dma_start(bo_sb[:], bo.unsqueeze(0).broadcast_to([P, DM])).then_inc(S["bo"], 16)
            sp.wait_ge(S["kl"], 1)
            sp.dma_start(k_dram.rearrange("t (c p) k -> p t c k", p=P), kpart[:]).then_inc(S["kwr"], 16)
            sp.wait_ge(S["kwr"], 16)
            for i, part in enumerate(KBLK):
                sp.dma_start(kst[i * DH:(i + 1) * DH],
                             k_dram[part].rearrange("(h d) k -> d h k", d=DH)).then_inc(S["krd"], 16)
            for b in range(4, B):
                sp.dma_start(x_sb[:, b], x_v[b]).then_inc(s_xload[b], 16)
            for step in STEPS:
                m, f = step + MAXI, step + FRONT
                if valid(m):
                    sp.wait_ge(S["nm_sb"], m + 1)
                    if m >= QRING:
                        sp.wait_ge(S["scores"], U * (m - QRING + 1))
                    for a in range(2):
                        sp.dma_start(qst[NBLK * DH + a:NBLK * DH + a + 1, m % QRING],
                                     nmaxT[a * HEADS:(a + 1) * HEADS, :]).then_inc(S["nmrow"], 16)
                if valid(f):
                    sp.wait_ge(S["ql"], f + 1)
                    sp.dma_start(q_dram[f].rearrange("t (c p) s -> p t c s", p=P), qpart[:, f % 2]).then_inc(s_qwr[f % 2], 16)
                    if f >= QRING:
                        sp.wait_ge(S["scores"], U * (f - QRING + 1))
                    sp.wait_ge(s_qwr[f % 2], 16 * (f // 2 + 1))
                    for i, part in enumerate(QBLK):
                        sp.dma_start(qst[i * DH:(i + 1) * DH, f % QRING],
                                     q_dram[f, part].rearrange("(h d) s -> d h s", d=DH)).then_inc(s_qrd[f % QRING], 16)
                if step == 0:
                    for c in range(C):
                        sp.dma_start(we_sb[:, c], expert_w[:, c * P:(c + 1) * P, :].rearrange("e p n -> p e n")).then_inc(S["we"], 16)
                    sp.dma_start(be_sb[:].rearrange("p e n -> p (e n)"),
                                 expert_b.rearrange("e n -> (e n)").unsqueeze(0).broadcast_to([P, NE * DM])).then_inc(S["be"], 16)
                if step == 2:
                    sp.wait_ge(S["zeros"], 1)
                    sp.dma_start(sorted_x.rearrange("(t p) d -> p t d", p=P),
                                 zeros.unsqueeze(1).broadcast_to([P, ST, DM])).then_inc(S["zfill"], 16)
            sp.wait_ge(S["scattered"], 16 * RT)
            for n in range(ST + XRING - 1):
                if n < ST:
                    if n >= XRING:
                        sp.wait_ge(S["xsT"], n - XRING + 1)
                    sp.dma_start(xs[n % XRING], sorted_x[n * P:(n + 1) * P, :]).then_inc(s_xs[n % XRING], 16)
                m = n - XRING + 1
                if m >= 0:
                    sp.wait_ge(S["y_sb"], m + 1)
                    sp.dma_start(sorted_y[m * P:(m + 1) * P, :], ys[m % YRING]).then_inc(s_ys[m % YRING], 16)
            for b in range(B):
                if b < RB:
                    sp.wait_ge(S["comb"], b + 1)
                else:
                    sp.wait_ge(S["acc"], 2 * NE * T * (b - RB + 1))
                sp.dma_start(out_v[b], x_sb[:, b]).then_inc(S["out"], 16)
            sp.wait_ge(S["out"], 16 * B)

        @block.gpsimd
        def _(pool):
            g = nc.gpsimd
            g.memset(ident[:], 0.0).then_inc(S["zeroed"], 1)
            g.memset(identb[:], 0.0).then_inc(S["zeroed"], 1)
            g.memset(minus_half[:], -0.5).then_inc(S["zeroed"], 1)
            pool.wait_ge(S["zeroed"], 3)
            for m in (ident, identb):
                g.affine_select(out=m[:], in_=m[:], compare_op=ALU.not_equal, fill=1.0, base=0,
                                pattern=[[-1, P]], channel_multiplier=1).then_inc(S["ident"], 1)
            g.iota(iota_e[:], pattern=[[1, NE]], base=0, channel_multiplier=0,
                   allow_small_or_imprecise_dtypes=True).then_inc(S["ident"], 1)

            g.memset(before_me[:], 1.0).then_inc(S["sort_c"], 1)
            g.memset(all_ones[:], 1.0).then_inc(S["sort_c"], 1)
            g.memset(upto[:], 1.0).then_inc(S["sort_c"], 1)
            g.memset(oh[:], 0.0).then_inc(S["oh_z"], 1)
            g.iota(iota_t[:], pattern=[[1, ST]], base=0, channel_multiplier=0,
                   allow_small_or_imprecise_dtypes=True).then_inc(S["sort_c"], 1)
            g.iota(iota_rows[:], pattern=[[P, RT]], base=0, channel_multiplier=0,
                   allow_small_or_imprecise_dtypes=True).then_inc(S["sort_c"], 1)
            pool.wait_ge(S["sort_c"], 5)
            g.affine_select(out=before_me[:], in_=before_me[:], compare_op=ALU.is_gt, fill=0.0, base=0,
                            pattern=[[1, P]], channel_multiplier=-1).then_inc(S["sort_c"], 1)
            g.affine_select(out=upto[:], in_=upto[:], compare_op=ALU.is_ge, fill=0.0, base=0,
                            pattern=[[1, NE], [-1, NE]], channel_multiplier=0).then_inc(S["sort_c"], 1)

            def norm1(b):
                pool.wait_ge(S["var1"], b + 1)
                g.tensor_tensor(rstd[:, b, :], mv[:, b, :, 1], minus_half[:], ALU.pow).then_inc(S["rstd1"], 1)
                pool.wait_ge(S["rstd1"], b + 1)
                if b >= 1:
                    pool.wait_ge(S["xT"], b)
                for i in range(T):
                    g.tensor_scalar(xn[:, i], x_sb[:, b, i], mv[:, b, i, 0:1], rstd[:, b, i:i + 1],
                                    ALU.add, ALU.mult).then_inc(S["xn1"], 1)

            norm1(0)
            g.memset(vaug[:], 0.0).then_inc(S["vaug_z"], 1)
            pool.wait_ge(S["vaug_z"], 1)
            g.memset(vaug[:, :, :, DH:DH + 1], 1.0).then_inc(S["vaug_set"], 1)

            for step in STEPS:
                k, f = step + BACK, step + FRONT
                if step >= 0 and valid(step):
                    pool.wait_ge(S["bo2"], 1)
                    pool.wait_ge(S["xn1"], T * (step + 1))
                    g.tensor_tensor(x_sb[:, step], x_sb[:, step], bo_sb[:].unsqueeze(1).broadcast_to([P, T, DM]),
                                    ALU.add).then_inc(S["xbias"], 1)
                if step == RB + 1:
                    pool.wait_ge(S["sortd"], 7)
                    pool.wait_ge(S["zfill"], 16)
                    pool.wait_ge(S["xn2"], RT)
                    for t in range(RT):
                        g.indirect_dma_start(sorted_x[:, :], bass.IndirectOffsetOnAxis(ap=row[:, t:t + 1].bitcast(U32), axis=0),
                                             xn2[:, t // T, t % T], None).then_inc(S["scattered"], 16)
                if valid(k):
                    pool.wait_ge(S["var2"], k + 1)
                    g.tensor_tensor(rstd2[:, k, :], mv2[:, k, :, 1], minus_half[:], ALU.pow).then_inc(S["rstd2"], 1)
                    pool.wait_ge(S["rstd2"], k + 1)
                    for i in range(T):
                        g.tensor_scalar(xn2[:, k, i], x_sb[:, k, i], mv2[:, k, i, 0:1], rstd2[:, k, i:i + 1],
                                        ALU.add, ALU.mult).then_inc(S["xn2"], 1)
                if valid(f):
                    pool.wait_ge(S["qm"], f + 1)
                    g.tensor_tensor(qpart[:, f % 2, 2], qr[:], qpart[:, f % 2, 1], ALU.subtract).then_inc(S["ql"], 1)
                if valid(f + 1):
                    norm1(f + 1)

            for n in range(YRING):
                pool.wait_ge(s_ys[n], 16 * len(range(n, ST, YRING)))
            pool.wait_ge(S["scattered"], 16 * RT)
            for t in range(RT):
                g.indirect_dma_start(xn2[:, t // T, t % T], None, sorted_y[:, :],
                                     bass.IndirectOffsetOnAxis(ap=row[:, t:t + 1].bitcast(U32), axis=0)).then_inc(s_back[t // T], 16)
            for b in range(RB):
                pool.wait_ge(S["gated"], T * (b + 1))
                g.tensor_tensor(x_sb[:, b], x_sb[:, b], xn2[:, b], ALU.add).then_inc(S["comb"], 1)

        @block.scalar
        def _(act):
            a = nc.scalar
            act.dma_start(ctx_sb[:], ctx_in.rearrange("b s d -> s b d")).then_inc(S["ctx"], 16)
            act.dma_start(wk_sb[:], wk.rearrange("(c p) n -> p c n", p=DCC)).then_inc(S["wk"], 16)
            for bias, bias_sb in ((bk, bk_sb), (bq, bq_sb), (bv, bv_sb)):
                act.dma_start(bias_sb[:], bias.rearrange("(c p) -> p c", p=P),
                              allow_slow_non_contiguous=True).then_inc(S["bcol"], 16)
            act.dma_start(wv_sb[:], wv.rearrange("(c p) n -> p c n", p=DCC)).then_inc(S["wv"], 16)
            act.dma_start(wr_sb[:], router_w.rearrange("(c p) n -> p c n", p=P)).then_inc(S["router"], 16)
            act.dma_start(br_sb[:], router_b.unsqueeze(0).broadcast_to([P, NE])).then_inc(S["router"], 16)
            act.wait_ge(S["bcol"], 48)
            a.mul(bq_s[:], bq_sb[:], SCALE).then_inc(S["bqs"], 1)
            a.copy(bv_bc[:], bv_sb[:].unsqueeze(2).broadcast_to([P, C, P])).then_inc(S["bvb"], 1)
            for n in range(4):
                c, half = n // 2, n % 2
                act.wait_ge(S["ctxT"], n + 1)
                a.copy(ctxT[:, c, half * HB * SK:(half + 1) * HB * SK],
                       bank[n][0:DCC, 0:HB * SK]).then_inc(S["ctxT_sb"], 1)
            kbanks = [*s_ps, *pv_ps]
            for n in range(4):
                half, m = n // 2, n % 2
                act.wait_ge(S["kT"], n + 1)
                a.activation(kT[:, m, half * HB * SK:(half + 1) * HB * SK], kbanks[n][:, 0:HB * SK], ACT.Identity,
                             bias=bk_sb[:, m:m + 1]).then_inc(S["kT_sb"], 1)
            act.wait_ge(S["kT_sb"], 4)
            a.copy(kpart[:, 0], kT[:]).then_inc(S["kh"], 1)
            act.wait_ge(S["bqs"], 1)

            def take_xT(b):
                act.wait_ge(S["xT"], b + 1)
                if b >= 1:
                    act.wait_ge(S["q"], b)
                a.copy(xnT[:].rearrange("p c s -> p (c s)"), bank_of["xT", b, 0][:]).then_inc(S["xT_sb"], 1)

            def take_q(b):
                act.wait_ge(S["q"], b + 1)
                if b >= 1:
                    act.wait_ge(S["qr"], b)
                for m in range(C):
                    a.activation(q32[:, m], bank_of["q", b, 0][:, m * SQ:(m + 1) * SQ], ACT.Identity,
                                 bias=bq_s[:, m:m + 1], scale=SCALE).then_inc(S["q_sb"], 1)
                act.wait_ge(S["q_sb"], C * (b + 1))
                if b >= 2:
                    act.wait_ge(s_qwr[b % 2], 16 * (b // 2))
                a.copy(qpart[:, b % 2, 0], q32[:]).then_inc(S["qh"], 1)

            def take_v(b):
                act.wait_ge(S["v"], b + 1)
                if b == 0:
                    act.wait_ge(S["vaug_set"], 1)
                a.copy(vaug[0:SK, b, :, 0:DH],
                       bank_of["v", b, 0][0:SK, 0:DM].rearrange("p (h e) -> p h e", e=DH)).then_inc(S["v_sb"], 1)

            def take_nm(b):
                act.wait_ge(S["nm"], b + 1)
                if b >= 1:
                    act.wait_ge(S["nmrow"], 32 * b)
                a.copy(nmaxT[:], bank_of["nm", b, 0][0:2 * HEADS, 0:P].bitcast(BF16)).then_inc(S["nm_sb"], 1)

            def take_pv(b, half):
                act.wait_ge(S["pv"], 4 * b + 2 * half + 2)
                if b >= 1:
                    act.wait_ge(S["oT"], T * b)
                a.copy(rawT[:, 2 * half:2 * half + 2, :].rearrange("p q s -> p (q s)"), pv_ps[half][:]).then_inc(S["pv_sb"], 1)

            def take_aT(b):
                act.wait_ge(S["aT"], b + 1)
                if b >= 1:
                    act.wait_ge(S["wo_ps"], b)
                a.copy(attnT[:].rearrange("p c s -> p (c s)"), bank_of["aT", b, 0][:]).then_inc(S["aT_sb"], 1)

            def take_x2T(b):
                act.wait_ge(S["x2T"], b + 1)
                if b >= 2:
                    act.wait_ge(S["lg_ps"], b - 1)
                a.copy(xn2T[:, :, b % 2, :],
                       bank_of["x2T", b, 0][:].rearrange("p (c s) -> p c s", c=C)).then_inc(S["x2T_sb"], 1)

            def take_xsT(n):
                act.wait_ge(S["xsT"], n + 1)
                if n >= 2:
                    act.wait_ge(S["y"], n - 1)
                a.copy(xsT[n % 2], s_ps[n % 2][:, 0:DM]).then_inc(S["xsT_sb"], 1)

            def exp_logits(t0, t1):
                act.wait_ge(S["rt"], 2 if t0 == 0 else 11)
                a.activation(elg[:, t0:t1], lgm[:, t0:t1], ACT.Exp).then_inc(S["elg"], 1)

            for step in STEPS:
                m, f, k = step + MAXI, step + FRONT, step + BACK
                for u in range(U):
                    if valid(step):
                        n = U * step + u
                        act.wait_ge(S["scores"], n + 1)
                        if n == 0:
                            act.wait_ge(S["probs_z"], 1)
                        if n >= 4:
                            act.wait_ge(S["pv"], (n - 4) // 2 + 1)
                        a.activation(probs[0:SK, n % 4].rearrange("p r s -> p (r s)"), s_ps[n % 2][0:SK, :],
                                     ACT.Exp).then_inc(S["exp"], 1)
                    if u == 0 and valid(k):
                        take_pv(k, 1)
                    if u == 0 and valid(k - 1) and step < B:
                        take_x2T(k - 1)
                    if u == 4:
                        if valid(step):
                            take_pv(step, 0)
                        if valid(k):
                            take_aT(k)
                        if valid(f):
                            take_v(f)
                    if u == 5 and valid(m):
                        take_nm(m)
                    if u == 6 and valid(f):
                        take_xT(f)
                    if u == 7 and valid(f):
                        take_q(f)
                    if step == RB + 1 and u == 6:
                        exp_logits(0, RT)
                    if (step, u) == (B, 7):
                        take_x2T(B - 2)
                    if (step, u) == (B + 1, 1):
                        take_x2T(B - 1)
                    for n in sorted_at(step, u):
                        if n == 0:
                            take_xsT(0)
                        if n + 1 < ST:
                            take_xsT(n + 1)
            exp_logits(RT, NT)
            act.wait_ge(S["rt"], 9)
            for t in range(RT):
                act.wait_ge(s_back[t // T], 16 * T)
                a.mul(xn2[:, t // T, t % T], xn2[:, t // T, t % T], gate[:, t:t + 1]).then_inc(S["gated"], 1)

        @block.vector
        def _(dve):
            v = nc.vector

            def moments(b, stats_, mv_, n):
                for i in range(T):
                    v.bn_stats(stats_[:, b, i, :], x_sb[:, b, i, :]).then_inc(S["bn" + n], 1)
                for i in range(T):
                    dve.wait_ge(S["bn" + n], T * b + i + 1)
                    v.bn_aggr(mv_[:, b, i, :], stats_[:, b, i, :]).then_inc(S["ag" + n], 1)
                dve.wait_ge(S["ag" + n], T * (b + 1))
                v.tensor_scalar(mv_[:, b, :, 1], mv_[:, b, :, 1], EPS, None, ALU.add)
                v.tensor_scalar(mv_[:, b, :, 0], mv_[:, b, :, 0], -1.0, None, ALU.mult).then_inc(S["var" + n], 1)

            def first_moments(b):
                dve.wait_ge(s_xload[b], 16)
                moments(b, stats, mv, "1")

            def key_parts():
                dve.wait_ge(S["kh"], 1)
                v.tensor_tensor(kr[:], kT[:], kpart[:, 0], ALU.subtract).then_inc(S["kr"], 1)
                dve.wait_ge(S["kr"], 1)
                v.tensor_copy(kpart[:, 1], kr[:]).then_inc(S["km"], 1)
                dve.wait_ge(S["km"], 1)
                v.tensor_tensor(kpart[:, 2], kr[:], kpart[:, 1], ALU.subtract).then_inc(S["kl"], 1)

            def query_parts(b):
                dve.wait_ge(S["qh"], b + 1)
                if b >= 1:
                    dve.wait_ge(S["ql"], b)
                v.tensor_tensor(qr[:], q32[:], qpart[:, b % 2, 0], ALU.subtract).then_inc(S["qr"], 1)
                dve.wait_ge(S["qr"], b + 1)
                v.tensor_copy(qpart[:, b % 2, 1], qr[:]).then_inc(S["qm"], 1)

            def maxima(b, parts):
                for k in parts:
                    i, grp = k // 4, k % 4
                    dve.wait_ge(S["mx"], 8 * b + k + 1)
                    if b >= 1 and k == 0:
                        dve.wait_ge(S["nml"], b)
                    v.tensor_reduce(smax[:, i, 4 * grp:4 * grp + 4],
                                    bank_of["mx", b, k][:, 0:4 * SK].rearrange("p (h k) -> p h k", k=SK),
                                    AX_X, ALU.max).then_inc(S["smax"], 1)

            def neg_max(b):
                dve.wait_ge(S["smax"], 8 * (b + 1))
                if b >= 1:
                    dve.wait_ge(S["nm"], b)
                v.tensor_scalar(nmax[:, :, 0:HEADS], smax[:], -1.0, None, ALU.mult).then_inc(S["nmh"], 1)
                dve.wait_ge(S["nmh"], b + 1)
                v.scalar_tensor_tensor(out=nmax[:, :, HEADS:2 * HEADS], in0=smax[:], scalar=-1.0,
                                       in1=nmax[:, :, 0:HEADS], op0=ALU.mult, op1=ALU.subtract).then_inc(S["nml"], 1)

            def divide(b):
                for i in range(T):
                    n = T * b + i
                    dve.wait_ge(S["oT"], n + 1)
                    heads = bank_of["oT", b, i][:].rearrange("p (h e) -> p h e", e=32)
                    if n >= T:
                        dve.wait_ge(S["onorm"], n - T + 1)
                    v.reciprocal(rden[:, i], heads[:, :, DH]).then_inc(S["rec"], 1)
                    dve.wait_ge(S["rec"], n + 1)
                    if b >= 1:
                        dve.wait_ge(S["aT"], b)
                    v.tensor_tensor(attn[:, i].rearrange("p (h e) -> p h e", e=DH), heads[:, :, 0:DH],
                                    rden[:, i].unsqueeze(2).broadcast_to([P, HEADS, DH]), ALU.mult).then_inc(S["onorm"], 1)

            def residual(b):
                dve.wait_ge(S["wo_ps"], b + 1)
                dve.wait_ge(S["xbias"], b + 1)
                v.tensor_tensor(x_sb[:, b], bank_of["wo", b, 0][:].rearrange("p (i d) -> p i d", i=T),
                                x_sb[:, b], ALU.add).then_inc(S["x2"], 1)
                dve.wait_ge(S["x2"], b + 1)
                moments(b, stats2, mv2, "2")

            def logits(b):
                dve.wait_ge(S["lg_ps"], b + 1)
                v.tensor_tensor(lg[:, T * b:T * b + T],
                                bank_of["lg", b, 0][:, 0:T * NE].rearrange("p (i e) -> p i e", i=T),
                                br_sb[:].unsqueeze(1).broadcast_to([P, T, NE]), ALU.add).then_inc(S["lg"], 1)

            def route(t0, t1, r):
                n = t1 - t0
                dve.wait_ge(S["lg"], t1 // T)
                dve.wait_ge(S["ident"], 3)
                v.tensor_reduce(lmx[:, t0:t1], lg[:, t0:t1], AX_X, ALU.max).then_inc(S["rt"], 1)
                dve.wait_ge(S["rt"], r + 1)
                v.tensor_tensor(lgm[:, t0:t1], lg[:, t0:t1], lmx[:, t0:t1].unsqueeze(2).broadcast_to([P, n, NE]),
                                ALU.subtract).then_inc(S["rt"], 1)
                dve.wait_ge(S["rt"], r + 2)
                v.tensor_scalar(cand[:, t0:t1], lgm[:, t0:t1], 0.0, float(NE), ALU.is_lt, ALU.mult).then_inc(S["rt"], 1)
                dve.wait_ge(S["rt"], r + 3)
                v.tensor_tensor(cand[:, t0:t1], cand[:, t0:t1], iota_e[:].unsqueeze(1).broadcast_to([P, n, NE]),
                                ALU.add).then_inc(S["rt"], 1)
                dve.wait_ge(S["rt"], r + 4)
                v.tensor_reduce(idx[:, t0:t1], cand[:, t0:t1], AX_X, ALU.min).then_inc(S["rt"], 1)
                dve.wait_ge(S["rt"], r + 5)
                v.tensor_tensor(ohg[:, t0:t1], cand[:, t0:t1], idx[:, t0:t1].unsqueeze(2).broadcast_to([P, n, NE]),
                                ALU.is_equal).then_inc(S["rt"], 1)
                dve.wait_ge(S["rt"], r + 6)

            def gates(t0, t1, r):
                dve.wait_ge(S["elg"], 1 if t0 == 0 else 2)
                v.tensor_reduce(gate[:, t0:t1], elg[:, t0:t1], AX_X, ALU.add).then_inc(S["rt"], 1)
                dve.wait_ge(S["rt"], r + 7 + (t0 == 0))
                v.reciprocal(gate[:, t0:t1], gate[:, t0:t1]).then_inc(S["rt"], 1)

            def sort():
                dve.wait_ge(S["oh_z"], 1)
                dve.wait_ge(S["sort_c"], 7)
                v.tensor_copy(oh[:, 0:RT], ohg[:, 0:RT]).then_inc(S["rt"], 1)
                dve.wait_ge(S["rank"], 1)
                rank = bank_of["rank", 0, 0][:, 0:(RT + 1) * NE].rearrange("p (t e) -> p t e", e=NE)
                v.tensor_tensor(over[:], rank[:, RT].unsqueeze(2).broadcast_to([P, NE, RT]),
                                iota_rows[:].unsqueeze(1).broadcast_to([P, NE, RT]), ALU.is_gt).then_inc(S["sortd"], 1)
                dve.wait_ge(S["sortd"], 1)
                v.tensor_reduce(tiles_of[:], over[:], AX_X, ALU.add).then_inc(S["sortd"], 1)
                dve.wait_ge(S["sortd"], 2)
                v.tensor_tensor(prefix[:], tiles_of[:].unsqueeze(1).broadcast_to([P, NE, NE]), upto[:],
                                ALU.mult).then_inc(S["sortd"], 1)
                dve.wait_ge(S["sortd"], 3)
                v.tensor_reduce(end_tile[:], prefix[:], AX_X, ALU.add).then_inc(S["sortd"], 1)
                dve.wait_ge(S["sortd"], 4)
                v.tensor_tensor(start_tile[:], end_tile[:], tiles_of[:], ALU.subtract).then_inc(S["st"], 1)
                dve.wait_ge(S["st"], 1)
                v.scalar_tensor_tensor(out=row_e[:], in0=start_tile[:].unsqueeze(1).broadcast_to([P, RT, NE]),
                                       scalar=float(P), in1=rank[:, 0:RT], op0=ALU.mult, op1=ALU.add).then_inc(S["sortd"], 1)
                dve.wait_ge(S["sortd"], 5)
                v.tensor_tensor(row_e[:], row_e[:], ohg[:, 0:RT], ALU.mult).then_inc(S["st"], 1)
                dve.wait_ge(S["st"], 2)
                v.tensor_reduce(row_f[:], row_e[:], AX_X, ALU.add).then_inc(S["sortd"], 1)
                dve.wait_ge(S["sortd"], 6)
                v.tensor_copy(row[:], row_f[:]).then_inc(S["sortd"], 1)
                v.tensor_tensor(past[:], iota_t[0:1].unsqueeze(2).broadcast_to([1, ST, NE]),
                                end_tile[0:1].unsqueeze(1).broadcast_to([1, ST, NE]), ALU.is_ge).then_inc(S["st"], 1)
                dve.wait_ge(S["st"], 3)
                v.tensor_reduce(exp_f[:], past[:], AX_X, ALU.add).then_inc(S["st"], 1)
                dve.wait_ge(S["st"], 4)
                v.tensor_scalar(exp_of[:], exp_f[:], float(NE - 1), None, ALU.min).then_inc(S["exp_of"], 1)

            def take_y(n):
                e = v.value_load(exp_of[0:1, n:n + 1], min_val=0, max_val=NE - 1)
                if n >= YRING:
                    dve.wait_ge(s_ys[n % YRING], 16 * (n // YRING))
                dve.wait_ge(S["y"], n + 1)
                v.tensor_tensor(ys[n % YRING].unsqueeze(1), pv_ps[n % 2][:, 0:DM].unsqueeze(1),
                                be_sb[:, bass.ds(e, 1), :], ALU.add).then_inc(S["y_sb"], 1)

            first_moments(0)
            v.memset(probs[64:P], 0.0).then_inc(S["probs_z"], 1)
            v.memset(kst[NBLK * DH:KROWS].rearrange("p h k -> p (h k)").bitcast(F32), TWO_BF16_ONES).then_inc(S["kst_ones"], 1)
            for step in STEPS:
                m, f, k = step + MAXI, step + FRONT, step + BACK
                if valid(m):
                    maxima(m, range(0, 5))
                if valid(k):
                    divide(k)
                if valid(k - 1) and step < B:
                    if k == 1:
                        dve.wait_ge(S["router"], 32)
                    logits(k - 1)
                if valid(m):
                    maxima(m, range(5, 8))
                    neg_max(m)
                if step == RB + 1:
                    route(0, RT, 0)
                    sort()
                if step == B:
                    dve.wait_ge(S["be"], 16)
                    dve.wait_ge(S["exp_of"], 1)
                    for u in range(6):
                        for n in sorted_at(step, u):
                            take_y(n)
                if valid(k):
                    residual(k)
                if step == RB + 1:
                    gates(0, RT, 0)
                if step == B:
                    for u in range(6, U):
                        for n in sorted_at(step, u):
                            take_y(n)
                if step == B + 1:
                    for u in range(U):
                        if u == 0:
                            logits(B - 2)
                        if u == 3:
                            logits(B - 1)
                        for n in sorted_at(step, u):
                            take_y(n)
                if f == 0:
                    key_parts()
                    dve.wait_ge(S["kl"], 1)
                    v.memset(zeros, 0.0).then_inc(S["zeros"], 1)
                if valid(f):
                    query_parts(f)
                if valid(f + 1):
                    first_moments(f + 1)
                if step == -2:
                    dve.wait_ge(S["bvo"], 1)
                    dve.wait_ge(S["bo"], 16)
                    v.tensor_tensor(bo_sb[:], bank_of["bvo", 0, 0][:, 0:DM], bo_sb[:], ALU.add).then_inc(S["bo2"], 1)

            route(RT, NT, 9)
            gates(RT, NT, 9)
            dve.wait_ge(S["rt"], 17)
            v.tensor_tensor(ohg[:, RT:NT], ohg[:, RT:NT], gate[:, RT:NT].unsqueeze(2).broadcast_to([P, NT - RT, NE]),
                            ALU.mult).then_inc(S["rt"], 1)
            dve.wait_ge(S["rt"], 18)
            n = 0
            for t in range(RT, NT):
                y = x_sb[:, t // T, t % T, :]
                for e in range(NE):
                    if n:
                        dve.wait_ge(S["acc"], n)
                    v.scalar_tensor_tensor(out=y, in0=be_sb[:, e, :], scalar=ohg[:, t, e:e + 1], in1=y,
                                           op0=ALU.mult, op1=ALU.add).then_inc(S["acc"], 1)
                    n += 1
                    g = (NE // 2) * (t - RT) + e // 2
                    dve.wait_ge(S["ffn"], g + 1)
                    dve.wait_ge(S["acc"], n)
                    v.scalar_tensor_tensor(out=y, in0=bank[g % NBANK][:, (e % 2) * DM:(e % 2 + 1) * DM],
                                           scalar=ohg[:, t, e:e + 1], in1=y,
                                           op0=ALU.mult, op1=ALU.add).then_inc(S["acc"], 1)
                    n += 1

        @block.tensor
        def _(pe):
            m_ = nc.tensor.matmul
            transpose = nc.tensor.transpose
            pe.wait_ge(S["ident"], 3)
            pe.wait_ge(S["ctx"], 16)
            for n in range(4):
                c, half = n // 2, n % 2
                for b in range(HB):
                    last = transpose(bank[n][0:DCC, b * SK:(b + 1) * SK],
                                     ctx_sb[:, half * HB + b, c * DCC:(c + 1) * DCC], ident[0:SK, 0:SK])
                last.then_inc(S["ctxT"], 1)
            kbanks = [*s_ps, *pv_ps]
            pe.wait_ge(S["wk"], 16)
            for n in range(4):
                half, m = n // 2, n % 2
                pe.wait_ge(S["ctxT_sb"], half + 3)
                for c in range(CC):
                    last = m_(kbanks[n][:, 0:HB * SK], wk_sb[:, c, m * P:(m + 1) * P],
                              ctxT[:, c, half * HB * SK:(half + 1) * HB * SK], start=(c == 0), stop=(c == CC - 1))
                last.then_inc(S["kT"], 1)
            pe.wait_ge(S["wv"], 16)
            pe.wait_ge(S["wq"], 16)
            pe.wait_ge(S["ctxT_sb"], 4)

            def job(j):
                kind, b, k = j
                dst = bank_of[j]
                if before[j] is not None:
                    pe.wait_ge(*freed_by(before[j]))
                if kind == "xT":
                    pe.wait_ge(S["xn1"], T * (b + 1))
                    for c in range(C):
                        for i in range(T):
                            last = transpose(dst[:, c * SQ + i * P:c * SQ + (i + 1) * P],
                                             xn[:, i, c * P:(c + 1) * P], ident[:])
                    last.then_inc(S["xT"], 1)
                elif kind == "q":
                    pe.wait_ge(S["xT_sb"], b + 1)
                    for m in range(C):
                        for c in range(C):
                            last = m_(dst[:, m * SQ:(m + 1) * SQ], wq_sb[:, c, m * P:(m + 1) * P],
                                      xnT[:, c, :], start=(c == 0), stop=(c == C - 1))
                    last.then_inc(S["q"], 1)
                elif kind == "v":
                    for c in range(CC):
                        last = m_(dst[0:SK, 0:DM], ctxT[:, c, b * SK:(b + 1) * SK], wv_sb[:, c, :],
                                  start=(c == 0), stop=(c == CC - 1))
                    last.then_inc(S["v"], 1)
                elif kind == "bvo":
                    pe.wait_ge(S["bvb"], 1)
                    pe.wait_ge(S["wo"], 16)
                    for c in range(C):
                        last = m_(dst[:, 0:DM], bv_bc[:, c], wo_sb[:, c], start=(c == 0), stop=(c == C - 1))
                    last.then_inc(S["bvo"], 1)
                elif kind == "mx":
                    i, h0 = k // 4, 4 * (k % 4)
                    pe.wait_ge(s_qrd[b % QRING], 16 * NBLK * (b // QRING + 1))
                    for j4 in range(4):
                        last = m_(dst[:, j4 * SK:(j4 + 1) * SK], qst[0:NBLK * DH, b % QRING, h0 + j4, i * P:(i + 1) * P],
                                  kst[0:NBLK * DH, h0 + j4, b * SK:(b + 1) * SK], start=True, stop=True)
                    last.then_inc(S["mx"], 1)
                elif kind == "nm":
                    pe.wait_ge(S["nml"], b + 1)
                    d = dst[0:2 * HEADS, 0:P].bitcast(BF16)
                    for i in range(T):
                        last = transpose(d[:, i * P:(i + 1) * P], nmax[:, i, :], identb[:])
                    last.then_inc(S["nm"], 1)
                elif kind == "oT":
                    pe.wait_ge(S["pv_sb"], 2 * (b + 1))
                    for q in range(4):
                        last = transpose(dst[:, q * P:(q + 1) * P], rawT[:, q, k * P:(k + 1) * P], ident[:])
                    last.then_inc(S["oT"], 1)
                elif kind == "aT":
                    pe.wait_ge(S["onorm"], T * (b + 1))
                    for c in range(C):
                        for i in range(T):
                            last = transpose(dst[:, c * SQ + i * P:c * SQ + (i + 1) * P],
                                             attn[:, i, c * P:(c + 1) * P], ident[:])
                    last.then_inc(S["aT"], 1)
                elif kind == "wo":
                    pe.wait_ge(S["aT_sb"], b + 1)
                    for i in range(T):
                        for c in range(C):
                            last = m_(dst[:, i * DM:(i + 1) * DM], attnT[:, c, i * P:(i + 1) * P], wo_sb[:, c, :],
                                      start=(c == 0), stop=(c == C - 1))
                    last.then_inc(S["wo_ps"], 1)
                elif kind == "x2T":
                    pe.wait_ge(S["xn2"], T * (b + 1))
                    for c in range(C):
                        for i in range(T):
                            last = transpose(dst[:, c * SQ + i * P:c * SQ + (i + 1) * P],
                                             xn2[:, b, i, c * P:(c + 1) * P], ident[:])
                    last.then_inc(S["x2T"], 1)
                elif kind == "rank":
                    pe.wait_ge(S["rt"], 7)
                    m_(dst[:, 0:(RT + 1) * NE], before_me[:], oh[:].rearrange("p t e -> p (t e)"), start=True, stop=False)
                    for t in range(RT):
                        last = m_(dst[:, (t + 1) * NE:(RT + 1) * NE], all_ones[:],
                                  oh[:, t].unsqueeze(1).broadcast_to([P, RT - t, NE]), start=False, stop=(t == RT - 1))
                    last.then_inc(S["rank"], 1)
                else:
                    pe.wait_ge(S["x2T_sb"], b + 1)
                    for i in range(T):
                        for c in range(C):
                            last = m_(dst[:, i * NE:(i + 1) * NE], xn2T[:, c, b % 2, i * P:(i + 1) * P],
                                      wr_sb[:, c, :], start=(c == 0), stop=(c == C - 1))
                    last.then_inc(S["lg_ps"], 1)

            def scores(b, u):
                n = U * b + u
                if n >= 2:
                    pe.wait_ge(S["exp"], n - 1)
                if u == 0:
                    pe.wait_ge(S["nmrow"], 32 * (b + 1))
                for r in range(2):
                    last = m_(s_ps[n % 2][0:SK, r * SQ:(r + 1) * SQ], kst[:, 2 * u + r, b * SK:(b + 1) * SK],
                              qst[:, b % QRING, 2 * u + r, :], start=True, stop=True)
                last.then_inc(S["scores"], 1)

            def weighted(g):
                b, q = g // 4, g % 4
                pe.wait_ge(S["exp"], 2 * g + 2)
                if g >= 4:
                    pe.wait_ge(S["pv_sb"], g // 2 - 1)
                for j in range(4):
                    last = m_(pv_ps[q // 2][32 * j:32 * j + 32, (q % 2) * SQ:(q % 2 + 1) * SQ], vaug[:, b, 4 * q + j, :],
                              probs[:, (2 * g + j // 2) % 4, j % 2, :], start=True, stop=True)
                last.then_inc(S["pv"], 1)

            def turn(n):
                pe.wait_ge(s_xs[n % XRING], 16 * (n // XRING + 1))
                if n >= 2:
                    pe.wait_ge(S["xsT_sb"], n - 1)
                for c in range(C):
                    last = transpose(s_ps[n % 2][:, c * P:(c + 1) * P],
                                     xs[n % XRING][:, c * P:(c + 1) * P], ident[:])
                last.then_inc(S["xsT"], 1)

            def expert(n):
                e = nc.tensor.value_load(exp_of[0:1, n:n + 1], min_val=0, max_val=NE - 1)
                pe.wait_ge(S["xsT_sb"], n + 1)
                if n >= 2:
                    pe.wait_ge(S["y_sb"], n - 1)
                for c in range(C):
                    last = m_(pv_ps[n % 2][:, 0:DM], xsT[n % 2][:, c * P:(c + 1) * P],
                              we_sb[:, c, bass.ds(e, 1), :], start=(c == 0), stop=(c == C - 1))
                last.then_inc(S["y"], 1)

            for step in STEPS:
                if step == -MAXI:
                    pe.wait_ge(S["krd"], 16 * NBLK)
                if step == 0:
                    pe.wait_ge(S["kst_ones"], 1)
                    pe.wait_ge(S["router"], 32)
                for u in range(U):
                    if valid(step):
                        scores(step, u)
                    g = 4 * step + u // 2 - 1
                    if u % 2 == 0 and 0 <= g < 4 * B:
                        weighted(g)
                    for j in jobs_at(step, u):
                        job(j)
                    for n in sorted_at(step, u):
                        if n == 0:
                            pe.wait_ge(S["we"], 16 * C)
                            pe.wait_ge(S["exp_of"], 1)
                            pe.wait_ge(S["pv_sb"], 2 * B)
                            turn(0)
                        if n + 1 < ST:
                            turn(n + 1)
                        expert(n)

            for n in range(1, NBANK + 1):
                pe.wait_ge(*freed_by(order[-n]))
            for t in range(RT, NT):
                for e2 in range(NE // 2):
                    g = (NE // 2) * (t - RT) + e2
                    if g >= NBANK:
                        pe.wait_ge(S["acc"], 4 * (g - NBANK) + 4)
                    for c in range(C):
                        last = m_(bank[g % NBANK][:], xn2T[:, c, t // T % 2, t % T * P:(t % T + 1) * P],
                                  we_sb[:, c, 2 * e2:2 * e2 + 2, :].rearrange("p e n -> p (e n)"),
                                  start=(c == 0), stop=(c == C - 1))
                    last.then_inc(S["ffn"], 1)


_INS = ['x', 'ctx_768', 'L0_xattn_Wq', 'L0_xattn_bq', 'L0_xattn_Wk', 'L0_xattn_bk', 'L0_xattn_Wv', 'L0_xattn_bv',
        'L0_xattn_Wo', 'L0_xattn_bo', 'L0_ffn_router_w', 'L0_ffn_router_b', 'L0_ffn_expert_w', 'L0_ffn_expert_b']
_OUTS = [((8, 256, 256), 'float32')]


def kernel(**inputs):
    import numpy as _np
    import concourse.bacc as _bacc
    from concourse import mybir as _mybir
    from concourse.bass_utils import run_bass_kernel_spmd as _run

    nc = _bacc.Bacc("TRN2", target_bir_lowering=False, num_devices=1)
    arrays, args = {}, []
    for name in _INS:
        a = _np.ascontiguousarray(inputs[name])
        arrays[f"in_{name}_dram"] = a
        args.append(nc.dram_tensor(f"in_{name}_dram", a.shape, _mybir.dt.from_np(a.dtype), kind="ExternalInput").ap())
    for i, (shape, dtype) in enumerate(_OUTS):
        dt = _mybir.dt.from_np(_np.dtype(dtype))
        args.append(nc.dram_tensor(f"out_{i}_dram", shape, dt, kind="ExternalOutput").ap())
    xattn_moe_kernel(nc, *args)
    r = _run(nc, [arrays], core_ids=[0])
    got = tuple(r.results[0][f"out_{i}_dram"] for i in range(len(_OUTS)))
    return got[0]
```

```python
from contextlib import ExitStack

import numpy as np

import concourse.bass as bass
from concourse import mybir

ALU = mybir.AluOpType
ACT = mybir.ActivationFunctionType
F32 = mybir.dt.float32
BF16 = mybir.dt.bfloat16
I32 = mybir.dt.int32
U32 = mybir.dt.uint32
AX_X = mybir.AxisListType.X

P = 128
TWO_BF16_ONES = float(np.array([0x3F803F80], np.uint32).view(np.float32)[0])




def xattn_moe_kernel(nc, x, ctx_in, wq, bq, wk, bk, wv, bv, wo, bo, router_w, router_b, expert_w, expert_b, out):
    B, SQ, DM = x.shape
    _, SK, DC = ctx_in.shape
    NE = router_w.shape[1]
    HEADS = 16
    DH = DM // HEADS
    C = DM // P
    HC = P // DH
    T = SQ // P
    NT = B * T
    CC = 2
    DCC = DC // CC
    U = HEADS // 2
    HB = B // 2
    EPS = 1e-5
    QBLK, KBLK = (0, 0, 0, 1, 1, 2), (0, 1, 2, 0, 1, 0)
    NBLK = len(QBLK)
    QRING = 4
    SCALE = DH ** -0.5
    RB = B - 2
    RT = RB * T
    ST = RT + NE - 1
    XRING, YRING = 6, 4
    assert DM == 256 and SQ == 256 and T == 2 and C == 2 and B % 2 == 0

    x_v = x.rearrange("b (p i) d -> b p i d", i=T)
    out_v = out.rearrange("b (p i) d -> b p i d", i=T)

    q_dram = nc.dram_tensor("q_parts", (B, 3, DM, SQ), BF16, kind="Internal").ap()
    sorted_x = nc.dram_tensor("sorted_x", (ST * P, DM), F32, kind="Internal").ap()
    sorted_y = nc.dram_tensor("sorted_y", (ST * P, DM), F32, kind="Internal").ap()
    k_dram = nc.dram_tensor("k_parts", (3, DM, B * SK), BF16, kind="Internal").ap()

    with ExitStack() as ctx:
        def sb(name, shape, dt=F32):
            return ctx.enter_context(nc.sbuf_tensor(name, shape, dt))

        def sem(name):
            return ctx.enter_context(nc.semaphore(name))

        NBANK = 4
        bank = [ctx.enter_context(nc.psum_tensor(f"bank{i}", [P, 512], F32)) for i in range(NBANK)]
        s_ps = [ctx.enter_context(nc.psum_tensor(f"s_ps{i}", [P, 512], F32)) for i in range(2)]
        pv_ps = [ctx.enter_context(nc.psum_tensor(f"pv_ps{i}", [P, 512], F32)) for i in range(2)]

        early = [*s_ps, *pv_ps]

        ident = sb("ident", [P, P])
        identb = sb("identb", [P, P], BF16)
        iota_e = sb("iota_e", [P, NE])
        minus_half = sb("minus_half", [P, T])
        before_me = sb("before_me", [P, P], BF16)
        all_ones = sb("all_ones", [P, P], BF16)
        upto = sb("upto", [P, NE, NE])
        iota_t = sb("iota_t", [P, ST])
        iota_rows = sb("iota_rows", [P, RT])
        wq_sb = sb("wq_sb", [P, C, DM])
        wk_sb = sb("wk_sb", [DCC, CC, DM])
        wv_sb = sb("wv_sb", [DCC, CC, DM])
        wo_sb = sb("wo_sb", [P, C, DM])
        wr_sb = sb("wr_sb", [P, C, NE])
        we_sb = sb("we_sb", [P, C, NE, DM])
        bq_sb = sb("bq_sb", [P, C])
        bq_s = sb("bq_s", [P, C])
        bk_sb = sb("bk_sb", [P, C])
        bv_sb = sb("bv_sb", [P, C])
        bv_bc = sb("bv_bc", [P, C, P])
        bo_sb = sb("bo_sb", [P, DM])
        br_sb = sb("br_sb", [P, NE])
        be_sb = sb("be_sb", [P, NE, DM])
        ctx_sb = sb("ctx_sb", [SK, B, DC])
        ctxT = sb("ctxT", [DCC, CC, B * SK])
        KROWS = NBLK * DH + 2
        kT = sb("kT", [P, C, B * SK])
        kr = sb("kr", [P, C, B * SK])
        kpart = sb("kpart", [P, 3, C, B * SK], BF16)
        kst = sb("kst", [KROWS, HEADS, B * SK], BF16)
        q32 = sb("q32", [P, C, SQ])
        qr = sb("qr", [P, C, SQ])
        qpart = sb("qpart", [P, 2, 3, C, SQ], BF16)
        qst = sb("qst", [KROWS, QRING, HEADS, SQ], BF16)
        vaug = sb("vaug", [P, B, HEADS, 32])
        x_sb = sb("x_sb", [P, B, T, DM])
        stats = sb("stats", [P, B, T, 6])
        mv = sb("mv", [P, B, T, 2])
        rstd = sb("rstd", [P, B, T])
        xn = sb("xn", [P, T, DM])
        xnT = sb("xnT", [P, C, SQ])
        smax = sb("smax", [P, T, HEADS])
        nmax = sb("nmax", [P, T, 2 * HEADS], BF16)
        nmaxT = sb("nmaxT", [2 * HEADS, SQ], BF16)
        probs = sb("probs", [P, 4, 2, SQ])
        rawT = sb("rawT", [P, 4, SQ])
        rden = sb("rden", [P, T, HEADS])
        attn = sb("attn", [P, T, DM])
        attnT = sb("attnT", [P, C, SQ])
        stats2 = sb("stats2", [P, B, T, 6])
        mv2 = sb("mv2", [P, B, T, 2])
        rstd2 = sb("rstd2", [P, B, T])
        xn2 = sb("xn2", [P, B, T, DM])
        xn2T = sb("xn2T", [P, C, 2, SQ])
        lg = sb("lg", [P, NT, NE])
        lgm = sb("lgm", [P, NT, NE])
        elg = sb("elg", [P, NT, NE])
        lmx = sb("lmx", [P, NT])
        idx = sb("idx", [P, NT])
        cand = sb("cand", [P, NT, NE])
        gate = sb("gate", [P, NT])
        ohg = sb("ohg", [P, NT, NE])
        oh = sb("oh", [P, RT + 1, NE], BF16)
        over = sb("over", [P, NE, RT])
        tiles_of = sb("tiles_of", [P, NE])
        prefix = sb("prefix", [P, NE, NE])
        end_tile = sb("end_tile", [P, NE])
        start_tile = sb("start_tile", [P, NE])
        row_e = sb("row_e", [P, RT, NE])
        row_f = sb("row_f", [P, RT])
        row = sb("row", [P, RT], I32)
        past = sb("past", [1, ST, NE])
        exp_f = sb("exp_f", [1, ST])
        exp_of = sb("exp_of", [1, ST], I32)
        zeros = kr[:, 0, 0:DM]
        xs = [kpart[:].rearrange("p t c k -> p (t c k)").bitcast(F32)[:, n * DM:(n + 1) * DM] for n in range(XRING)]
        ys = [kT[:].rearrange("p c k -> p (c k)")[:, n * DM:(n + 1) * DM] for n in range(YRING)]
        xsT = [qr[:, n] for n in range(2)]

        names = ("zeroed ident vaug_z vaug_set kst_ones probs_z wq wk wv bk bq bv wo bo router we be bqs bvb "
                 "ctxT ctxT_sb kT kT_sb kh kr km kl xT xT_sb q q_sb qh qr qm ql nmrow "
                 "v v_sb bn1 ag1 var1 rstd1 xn1 bvo bo2 xbias mx smax nmh nml nm nm_sb "
                 "scores exp pv pv_sb oT rec onorm aT aT_sb wo_ps x2 bn2 ag2 var2 rstd2 xn2 x2T x2T_sb "
                 "lg_ps lg oh all acc out "
                 "sort_c oh_z zeros zfill rank sortd st exp_of scattered xsT xsT_sb y y_sb comb").split()
        S = {n: sem("s_" + n) for n in names}
        s_qwr = [sem(f"s_qwr{i}") for i in range(2)]
        s_q0 = [sem(f"s_q0_{i}") for i in range(3)]
        s_k0 = [sem(f"s_k0_{i}") for i in range(3)]
        s_qrd = [sem(f"s_qrd{i}") for i in range(QRING)]
        s_ctx = [sem(f"s_ctx{i}") for i in range(2)]
        s_kwr = sem("s_kwr1")
        s_krd = [sem(f"s_krd{i}") for i in range(2)]
        s_xs = [sem(f"s_xs{i}") for i in range(XRING)]
        s_ys = [sem(f"s_ys{i}") for i in range(YRING)]
        s_back = [sem(f"s_back{b}") for b in range(RB)]
        s_biased = [sem(f"s_biased{i}") for i in range(NT - RT)]
        s_rt = [sem(f"s_rt{i}") for i in range(3)]
        s_gate = [sem(f"s_gate{i}") for i in range(3)]
        s_elg = [sem(f"s_elg{i}") for i in range(3)]

        def group(t0):
            return 0 if t0 == 0 else 1 + (t0 - RT) // T

        s_xload = [sem(f"s_xload{b}") for b in range(B)]

        FRONT, MAXI, BACK = 3, 1, -1
        STEPS = range(-FRONT, B)

        def valid(b):
            return 0 <= b < B

        def jobs_at(step, u):
            m, f, k = step + MAXI, step + FRONT, step + BACK
            plan = {
                0: [("mx", m, i) for i in range(4)],
                1: [("mx", m, i) for i in range(4, 8)],
                2: [("nm", m, 0), ("xT", f, 0)],
                3: [("v", f, 0)],
            }.get(u, []) if step == -MAXI else {
                0: [("q", f - 1, 0), ("mx", m, 0)],
                1: [("mx", m, 1), ("mx", m, 2)],
                2: [("mx", m, 3), ("mx", m, 4), ("xT", f, 0)],
                3: [("mx", m, 5), ("mx", m, 6)],
                4: [("mx", m, 7)],
                5: [("nm", m, 0), ("q", f, 0)],
                6: [("v", f, 0)],
            }.get(u, []) if step == 0 else {
                0: [*([("x2T", k - 1, 0)] if step == RB + 1 else []), ("mx", m, 0), ("mx", m, 1)],
                1: [*([("lg", k - 1, 0)] if step == RB + 1 else []), ("xT", f, 0), ("mx", m, 2), ("mx", m, 3)],
                2: [("oT", k, 0), ("oT", k, 1), *([("x2T", k - 1, 0)] if step != RB + 1 else [])],
                3: [("q", f, 0), ("mx", m, 4), ("mx", m, 5)] + [("rank", 0, 0)] * (step == RB + 1),
                4: [("aT", k, 0), ("mx", m, 6), ("mx", m, 7), *([("lg", k - 1, 0)] if step != RB + 1 else [])],
                5: [("nm", m, 0), ("wo", k, 0)],
                6: [("v", f, 0)] + ([("bvo", step + 2, 0)] if step == -2 else []),
                7: [],
            }[u]
            return [j for j in plan if valid(j[1])]

        G = NE // 2
        E, L = B - 2, B - 1
        EARLY = 6
        TAIL = [("oT", L, 0), ("oT", L, 1), ("x2T", E, 0), ("lg", E, 0), ("all", 0, 0), ("aT", L, 0), ("all", 1, 0),
                ("wo", L, 0), *[("all", g, 0) for g in range(2, EARLY)], *[("tile", n, 0) for n in range(4)],
                ("x2T", L, 0), ("tile", 4, 0), ("tile", 5, 0), ("lg", L, 0), *[("tile", n, 0) for n in range(6, ST)],
                *[("all", g, 0) for g in range(EARLY, 2 * G * T)]]

        def biases_at(j):
            kind, n, _ = j
            if kind == "all" and n < G:
                return [(RT + 1, 2 * n), (RT + 1, 2 * n + 1)]
            if kind == "all" and n < 2 * G:
                return [(RT, 2 * (n - G)), (RT, 2 * (n - G) + 1)]
            if kind == "tile" and 6 <= n < 6 + NE:
                return [(RT + 2, n - 6)]
            if kind == "tile" and n >= 6 + NE:
                return [(RT + 3, n - 6 - NE)]
            late = ST - 6 - NE + n - 2 * G
            if kind == "all" and 2 * G <= n and late < NE:
                return [(RT + 3, late)]
            return []

        order = [j for step in STEPS for u in range(U) for j in jobs_at(step, u)]
        order += [j for j in TAIL if j[0] != "tile"]
        bank_of = {j: bank[n % NBANK] for n, j in enumerate(order)}
        before = {j: (order[n - NBANK] if n >= NBANK else None) for n, j in enumerate(order)}

        def freed_by(job):
            kind, b, k = job
            return {"mx": (S["smax"], 8 * b + k + 1), "nm": (S["nm_sb"], b + 1), "wo": (S["x2"], b + 1),
                    "x2T": (S["x2T_sb"], b + 1), "lg": (S["lg"], b + 1), "oT": (S["onorm"], T * b + k + 1),
                    "aT": (S["aT_sb"], b + 1), "xT": (S["xT_sb"], b + 1), "q": (S["q_sb"], C * (b + 1)),
                    "v": (S["v_sb"], b + 1), "rank": (S["sortd"], 5), "all": (S["acc"], 2 * (b + 1)),
                    "bvo": (S["bo2"], 1)}[kind]

        def half_keys(half):
            return slice(half * HB * SK, (half + 1) * HB * SK)

        block = ctx.enter_context(nc.Block())

        @block.sync
        def _(sp):
            ready_q, ready_k = [S[n] for n in ("qh", "qm", "ql")], [S[n] for n in ("kh", "km", "kl")]

            def key_part_out(half, t):
                ks = half_keys(half)
                sp.wait_ge(ready_k[t], half + 1)
                sp.dma_start(k_dram[t, :, ks].rearrange("(c p) k -> p c k", p=P), kpart[:, t, :, ks]).then_inc(
                    s_k0[t] if half == 0 else s_kwr, 16)

            def key_part_back(half, t):
                ks = half_keys(half)
                for i, part in enumerate(KBLK):
                    if part == t:
                        sp.dma_start(kst[i * DH:(i + 1) * DH, :, ks],
                                     k_dram[part, :, ks].rearrange("(h d) k -> d h k", d=DH)).then_inc(s_krd[half], 16)

            def first_parts():
                def query_out(t):
                    sp.wait_ge(ready_q[t], 1)
                    sp.dma_start(q_dram[0, t].rearrange("(c p) s -> p c s", p=P), qpart[:, 0, t]).then_inc(s_q0[t], 16)

                def query_back(t):
                    sp.wait_ge(s_q0[t], 16)
                    for i, part in enumerate(QBLK):
                        if part == t:
                            sp.dma_start(qst[i * DH:(i + 1) * DH, 0],
                                         q_dram[0, part].rearrange("(h d) s -> d h s", d=DH)).then_inc(s_qrd[0], 16)

                query_out(0)
                query_out(1)
                query_out(2)
                query_back(0)
                key_part_out(0, 0)
                query_back(1)
                key_part_out(0, 1)
                query_back(2)
                key_part_out(0, 2)
                for t in range(3):
                    sp.wait_ge(s_k0[t], 16)
                    key_part_back(0, t)

            sp.dma_start(x_sb[:, 0], x_v[0]).then_inc(s_xload[0], 16)
            sp.dma_start(wq_sb[:], wq.rearrange("(c p) n -> p c n", p=P)).then_inc(S["wq"], 16)
            sp.dma_start(bq_sb[:], bq.rearrange("(c p) -> p c", p=P), allow_slow_non_contiguous=True).then_inc(S["bq"], 16)
            sp.dma_start(x_sb[:, 1], x_v[1]).then_inc(s_xload[1], 16)
            sp.dma_start(bk_sb[:], bk.rearrange("(c p) -> p c", p=P), allow_slow_non_contiguous=True).then_inc(S["bk"], 16)
            sp.dma_start(bv_sb[:], bv.rearrange("(c p) -> p c", p=P), allow_slow_non_contiguous=True).then_inc(S["bv"], 16)
            sp.dma_start(wv_sb[:], wv.rearrange("(c p) n -> p c n", p=DCC)).then_inc(S["wv"], 16)
            sp.dma_start(wo_sb[:], wo.rearrange("(c p) n -> p c n", p=P)).then_inc(S["wo"], 16)
            sp.dma_start(bo_sb[:], bo.unsqueeze(0).broadcast_to([P, DM])).then_inc(S["bo"], 16)
            for b in range(2, 4):
                sp.dma_start(x_sb[:, b], x_v[b]).then_inc(s_xload[b], 16)
            sp.dma_start(wr_sb[:], router_w.rearrange("(c p) n -> p c n", p=P)).then_inc(S["router"], 16)
            sp.dma_start(br_sb[:], router_b.unsqueeze(0).broadcast_to([P, NE])).then_inc(S["router"], 16)
            for step in STEPS:
                f = step + FRONT
                if f == 0:
                    first_parts()
                elif valid(f):
                    sp.wait_ge(S["ql"], f + 1)
                    sp.dma_start(q_dram[f].rearrange("t (c p) s -> p t c s", p=P), qpart[:, f % 2]).then_inc(s_qwr[f % 2], 16)
                    if f >= QRING:
                        sp.wait_ge(S["scores"], U * (f - QRING + 1))
                    sp.wait_ge(s_qwr[f % 2], 16 * ((f + 1) // 2))
                    for i, part in enumerate(QBLK):
                        sp.dma_start(qst[i * DH:(i + 1) * DH, f % QRING],
                                     q_dram[f, part].rearrange("(h d) s -> d h s", d=DH)).then_inc(s_qrd[f % QRING], 16)
                if f == FRONT:
                    for t in range(3):
                        key_part_out(1, t)
                    sp.wait_ge(s_kwr, 48)
                    for t in range(3):
                        key_part_back(1, t)
                if 1 <= f and f + 3 < B:
                    sp.dma_start(x_sb[:, f + 3], x_v[f + 3]).then_inc(s_xload[f + 3], 16)
                e = step + 1
                if 0 <= e < NE:
                    sp.dma_start(we_sb[:, :, e], expert_w[e].rearrange("(c p) n -> p c n", p=P)).then_inc(S["we"], 16)
                    sp.dma_start(be_sb[:, e], expert_b[e:e + 1].broadcast_to([P, DM])).then_inc(S["be"], 16)
                    t0, t1 = -(-ST * e // NE), -(-ST * (e + 1) // NE)
                    if e == 0:
                        sp.wait_ge(S["zeros"], 1)
                    sp.dma_start(sorted_x.rearrange("(t p) d -> p t d", p=P)[:, t0:t1],
                                 zeros.unsqueeze(1).broadcast_to([P, t1 - t0, DM])).then_inc(S["zfill"], 16)
            sp.wait_ge(S["scattered"], 16 * RT)
            for n in range(ST + XRING - 1):
                if n < ST:
                    if n >= XRING:
                        sp.wait_ge(S["xsT"], n - XRING + 1)
                    sp.dma_start(xs[n % XRING], sorted_x[n * P:(n + 1) * P, :]).then_inc(s_xs[n % XRING], 16)
                m = n - XRING + 1
                if m >= 0:
                    sp.wait_ge(S["y_sb"], m + 1)
                    sp.dma_start(sorted_y[m * P:(m + 1) * P, :], ys[m % YRING]).then_inc(s_ys[m % YRING], 16)
            sp.wait_ge(S["acc"], NE * T)
            sp.wait_ge(s_biased[0], NE)
            sp.dma_start(out_v[E], x_sb[:, E]).then_inc(S["out"], 16)
            last_sorted = [(RB - 1, i) for i in range(T)]
            for b, i in ((0, None), (1, None), (L, 0), *[(b, None) for b in range(2, RB - 1)], *last_sorted, (L, 1)):
                if b == L:
                    sp.wait_ge(S["acc"], NE * (T + i + 1))
                elif i is None:
                    sp.wait_ge(S["comb"], T * (b + 1))
                else:
                    sp.wait_ge(S["comb"], T * b + i + 1)
                if i is None:
                    sp.dma_start(out_v[b], x_sb[:, b]).then_inc(S["out"], 16)
                else:
                    sp.dma_start(out_v[b][:, i], x_sb[:, b, i]).then_inc(S["out"], 16)
            sp.wait_ge(S["out"], 16 * (B - 2 + 2 * T))

        @block.gpsimd
        def _(pool):
            g = nc.gpsimd
            g.memset(ident[:], 0.0).then_inc(S["zeroed"], 1)
            g.memset(identb[:], 0.0).then_inc(S["zeroed"], 1)
            g.memset(minus_half[:], -0.5).then_inc(S["zeroed"], 1)
            pool.wait_ge(S["zeroed"], 3)
            for m in (ident, identb):
                g.affine_select(out=m[:], in_=m[:], compare_op=ALU.not_equal, fill=1.0, base=0,
                                pattern=[[-1, P]], channel_multiplier=1).then_inc(S["ident"], 1)
            g.iota(iota_e[:], pattern=[[1, NE]], base=0, channel_multiplier=0,
                   allow_small_or_imprecise_dtypes=True).then_inc(S["ident"], 1)

            g.memset(before_me[:], 1.0).then_inc(S["sort_c"], 1)
            g.memset(all_ones[:], 1.0).then_inc(S["sort_c"], 1)
            g.memset(upto[:], 1.0).then_inc(S["sort_c"], 1)
            g.memset(oh[:], 0.0).then_inc(S["oh_z"], 1)
            g.iota(iota_t[:], pattern=[[1, ST]], base=0, channel_multiplier=0,
                   allow_small_or_imprecise_dtypes=True).then_inc(S["sort_c"], 1)
            g.iota(iota_rows[:], pattern=[[P, RT]], base=0, channel_multiplier=0,
                   allow_small_or_imprecise_dtypes=True).then_inc(S["sort_c"], 1)
            pool.wait_ge(S["sort_c"], 5)
            g.affine_select(out=before_me[:], in_=before_me[:], compare_op=ALU.is_gt, fill=0.0, base=0,
                            pattern=[[1, P]], channel_multiplier=-1).then_inc(S["sort_c"], 1)
            g.affine_select(out=upto[:], in_=upto[:], compare_op=ALU.is_ge, fill=0.0, base=0,
                            pattern=[[1, NE], [-1, NE]], channel_multiplier=0).then_inc(S["sort_c"], 1)

            def norm1(b):
                pool.wait_ge(S["var1"], b + 1)
                g.tensor_tensor(rstd[:, b, :], mv[:, b, :, 1], minus_half[:], ALU.pow).then_inc(S["rstd1"], 1)
                pool.wait_ge(S["rstd1"], b + 1)
                if b >= 1:
                    pool.wait_ge(S["xT"], b)
                for i in range(T):
                    g.tensor_scalar(xn[:, i], x_sb[:, b, i], mv[:, b, i, 0:1], rstd[:, b, i:i + 1],
                                    ALU.add, ALU.mult).then_inc(S["xn1"], 1)

            def norm2(k):
                pool.wait_ge(S["var2"], k + 1)
                g.tensor_tensor(rstd2[:, k, :], mv2[:, k, :, 1], minus_half[:], ALU.pow).then_inc(S["rstd2"], 1)
                pool.wait_ge(S["rstd2"], k + 1)
                for i in range(T):
                    g.tensor_scalar(xn2[:, k, i], x_sb[:, k, i], mv2[:, k, i, 0:1], rstd2[:, k, i:i + 1],
                                    ALU.add, ALU.mult).then_inc(S["xn2"], 1)

            norm1(0)
            g.memset(vaug[:], 0.0).then_inc(S["vaug_z"], 1)
            pool.wait_ge(S["vaug_z"], 1)
            g.memset(vaug[:, :, :, DH:DH + 1], 1.0).then_inc(S["vaug_set"], 1)

            for step in STEPS:
                k, f = step + BACK, step + FRONT
                if step >= 0 and valid(step):
                    pool.wait_ge(S["bo2"], 1)
                    pool.wait_ge(S["xn1"], T * (step + 1))
                    g.tensor_tensor(x_sb[:, step], x_sb[:, step], bo_sb[:].unsqueeze(1).broadcast_to([P, T, DM]),
                                    ALU.add).then_inc(S["xbias"], 1)
                if valid(f + 1):
                    norm1(f + 1)
                if valid(f):
                    pool.wait_ge(S["qm"], f + 1)
                    g.tensor_tensor(qpart[:, f % 2, 2], qr[:], qpart[:, f % 2, 1], ALU.subtract).then_inc(S["ql"], 1)
                if f == 1:
                    pool.wait_ge(S["ql"], f + 1)
                    pool.wait_ge(S["xn1"], T * (f + 2))
                    pool.wait_ge(S["vaug_set"], 1)
                    g.memset(kst[NBLK * DH:KROWS].rearrange("p h k -> p (h k)").bitcast(F32), TWO_BF16_ONES).then_inc(S["kst_ones"], 1)
                    pool.wait_ge(S["kst_ones"], 1)
                if valid(k) and k < E:
                    norm2(k)

            pool.wait_ge(S["sortd"], 7)
            pool.wait_ge(S["zfill"], 16 * NE)
            pool.wait_ge(S["xn2"], RT)
            for t in range(RT):
                if t == 4:
                    norm2(E)
                g.indirect_dma_start(sorted_x[:, :], bass.IndirectOffsetOnAxis(ap=row[:, t:t + 1].bitcast(U32), axis=0),
                                     xn2[:, t // T, t % T], None).then_inc(S["scattered"], 16)
            norm2(L)
            for n in range(YRING):
                pool.wait_ge(s_ys[n], 16 * len(range(n, ST, YRING)))
            pool.wait_ge(S["scattered"], 16 * RT)
            for t in range(RT):
                g.indirect_dma_start(xn2[:, t // T, t % T], None, sorted_y[:, :],
                                     bass.IndirectOffsetOnAxis(ap=row[:, t:t + 1].bitcast(U32), axis=0)).then_inc(s_back[t // T], 16)

        @block.scalar
        def _(act):
            a = nc.scalar
            act.dma_start(ctx_sb[:, 0:HB], ctx_in[0:HB].rearrange("b s d -> s b d")).then_inc(s_ctx[0], 16)
            act.dma_start(wk_sb[:], wk.rearrange("(c p) n -> p c n", p=DCC)).then_inc(S["wk"], 16)
            act.dma_start(ctx_sb[:, HB:B], ctx_in[HB:B].rearrange("b s d -> s b d")).then_inc(s_ctx[1], 16)
            for n in range(4):
                half, c = n // 2, n % 2
                act.wait_ge(S["ctxT"], n + 1)
                a.copy(ctxT[:, c, half_keys(half)], early[n][0:DCC, 0:HB * SK]).then_inc(S["ctxT_sb"], 1)

            def take_keys(half):
                act.wait_ge(S["bk"], 16)
                for m in range(C):
                    act.wait_ge(S["kT"], C * half + m + 1)
                    a.activation(kT[:, m, half_keys(half)], early[C * half + m][:, 0:HB * SK], ACT.Identity,
                                 bias=bk_sb[:, m:m + 1]).then_inc(S["kT_sb"], 1)
                act.wait_ge(S["kT_sb"], C * (half + 1))
                a.copy(kpart[:, 0, :, half_keys(half)], kT[:, :, half_keys(half)]).then_inc(S["kh"], 1)

            act.wait_ge(S["bq"], 16)
            a.mul(bq_s[:], bq_sb[:], SCALE).then_inc(S["bqs"], 1)
            act.wait_ge(S["bqs"], 1)

            def take_xT(b):
                act.wait_ge(S["xT"], b + 1)
                if b >= 1:
                    act.wait_ge(S["q"], b)
                a.copy(xnT[:].rearrange("p c s -> p (c s)"), bank_of["xT", b, 0][:]).then_inc(S["xT_sb"], 1)

            def take_q(b):
                act.wait_ge(S["q"], b + 1)
                if b >= 1:
                    act.wait_ge(S["qr"], b)
                for m in range(C):
                    a.activation(q32[:, m], bank_of["q", b, 0][:, m * SQ:(m + 1) * SQ], ACT.Identity,
                                 bias=bq_s[:, m:m + 1], scale=SCALE).then_inc(S["q_sb"], 1)
                act.wait_ge(S["q_sb"], C * (b + 1))
                if b >= 2:
                    act.wait_ge(s_qwr[b % 2], 16 * ((b - 1) // 2))
                if b == 2:
                    for t in range(3):
                        act.wait_ge(s_q0[t], 16)
                a.copy(qpart[:, b % 2, 0], q32[:]).then_inc(S["qh"], 1)

            def take_v(b):
                act.wait_ge(S["v"], b + 1)
                if b == 0:
                    act.wait_ge(S["vaug_set"], 1)
                a.copy(vaug[0:SK, b, :, 0:DH],
                       bank_of["v", b, 0][0:SK, 0:DM].rearrange("p (h e) -> p h e", e=DH)).then_inc(S["v_sb"], 1)

            def take_nm(b):
                act.wait_ge(S["nm"], b + 1)
                if b >= 1:
                    act.wait_ge(S["nmrow"], 32 * b)
                a.copy(nmaxT[:], bank_of["nm", b, 0][0:2 * HEADS, 0:P].bitcast(BF16)).then_inc(S["nm_sb"], 1)
                act.wait_ge(S["nm_sb"], b + 1)
                if b >= QRING:
                    act.wait_ge(S["scores"], U * (b - QRING + 1))
                for i in range(2):
                    act.dma_start(qst[NBLK * DH + i:NBLK * DH + i + 1, b % QRING],
                                  nmaxT[i * HEADS:(i + 1) * HEADS, :]).then_inc(S["nmrow"], 16)

            def take_pv(b, half):
                act.wait_ge(S["pv"], 4 * b + 2 * half + 2)
                if b >= 1:
                    act.wait_ge(S["oT"], T * b)
                a.copy(rawT[:, 2 * half:2 * half + 2, :].rearrange("p q s -> p (q s)"), pv_ps[half][:]).then_inc(S["pv_sb"], 1)

            def take_aT(b):
                act.wait_ge(S["aT"], b + 1)
                if b >= 1:
                    act.wait_ge(S["wo_ps"], b)
                a.copy(attnT[:].rearrange("p c s -> p (c s)"), bank_of["aT", b, 0][:]).then_inc(S["aT_sb"], 1)

            def take_x2T(b):
                act.wait_ge(S["x2T"], b + 1)
                if b >= 2:
                    act.wait_ge(S["lg_ps"], b - 1)
                a.copy(xn2T[:, :, b % 2, :],
                       bank_of["x2T", b, 0][:].rearrange("p (c s) -> p c s", c=C)).then_inc(S["x2T_sb"], 1)

            def take_xsT(n):
                act.wait_ge(S["xsT"], n + 1)
                if n >= 2:
                    act.wait_ge(S["y"], n - 1)
                a.copy(xsT[n % 2], s_ps[n % 2][:, 0:DM]).then_inc(S["xsT_sb"], 1)

            def exp_logits(t0, t1):
                act.wait_ge(s_rt[group(t0)], 2)
                a.activation(elg[:, t0:t1], lgm[:, t0:t1], ACT.Exp).then_inc(s_elg[group(t0)], 1)

            take = {"x2T": take_x2T, "xT": take_xT, "v": take_v, "q": take_q, "aT": take_aT, "nm": take_nm}
            for step in STEPS:
                k = step + BACK
                if step == 1 - FRONT:
                    take_keys(0)
                    act.wait_ge(S["bv"], 16)
                    a.copy(bv_bc[:], bv_sb[:].unsqueeze(2).broadcast_to([P, C, P])).then_inc(S["bvb"], 1)
                if step == -MAXI:
                    take_keys(1)
                for u in range(U):
                    if valid(step):
                        n = U * step + u
                        act.wait_ge(S["scores"], n + 1)
                        if n == 0:
                            act.wait_ge(S["probs_z"], 1)
                        if n >= 4:
                            act.wait_ge(S["pv"], (n - 4) // 2 + 1)
                        a.activation(probs[0:SK, n % 4].rearrange("p r s -> p (r s)"), s_ps[n % 2][0:SK, :],
                                     ACT.Exp).then_inc(S["exp"], 1)
                    if u == 0 and valid(k):
                        take_pv(k, 1)
                    if u == 4 and valid(step):
                        take_pv(step, 0)
                    for kind, b, _ in jobs_at(step, u):
                        if kind in take:
                            take[kind](b)
                    if step == RB + 1 and u == 6:
                        exp_logits(0, RT)
            take_pv(L, 1)
            for j in TAIL:
                kind, n, _ = j
                if kind == "x2T":
                    take_x2T(n)
                elif kind == "aT":
                    take_aT(n)
                elif j == ("lg", E, 0):
                    exp_logits(RT, RT + T)
                elif j == ("tile", 6, 0):
                    exp_logits(RT + T, NT)
                if kind == "tile":
                    if n == 0:
                        take_xsT(0)
                    if n + 1 < ST:
                        take_xsT(n + 1)

        @block.vector
        def _(dve):
            v = nc.vector

            def moments(b, stats_, mv_, n):
                for i in range(T):
                    v.bn_stats(stats_[:, b, i, :], x_sb[:, b, i, :]).then_inc(S["bn" + n], 1)
                for i in range(T):
                    dve.wait_ge(S["bn" + n], T * b + i + 1)
                    v.bn_aggr(mv_[:, b, i, :], stats_[:, b, i, :]).then_inc(S["ag" + n], 1)
                dve.wait_ge(S["ag" + n], T * (b + 1))
                v.tensor_scalar(mv_[:, b, :, 1], mv_[:, b, :, 1], EPS, None, ALU.add)
                v.tensor_scalar(mv_[:, b, :, 0], mv_[:, b, :, 0], -1.0, None, ALU.mult).then_inc(S["var" + n], 1)

            def first_moments(b):
                dve.wait_ge(s_xload[b], 16)
                moments(b, stats, mv, "1")

            def key_parts(half):
                ks = half_keys(half)
                dve.wait_ge(S["kh"], half + 1)
                v.tensor_tensor(kr[:, :, ks], kT[:, :, ks], kpart[:, 0, :, ks], ALU.subtract).then_inc(S["kr"], 1)
                dve.wait_ge(S["kr"], half + 1)
                v.tensor_copy(kpart[:, 1, :, ks], kr[:, :, ks]).then_inc(S["km"], 1)
                dve.wait_ge(S["km"], half + 1)
                v.tensor_tensor(kpart[:, 2, :, ks], kr[:, :, ks], kpart[:, 1, :, ks], ALU.subtract).then_inc(S["kl"], 1)

            def query_parts(b):
                dve.wait_ge(S["qh"], b + 1)
                if b >= 1:
                    dve.wait_ge(S["ql"], b)
                v.tensor_tensor(qr[:], q32[:], qpart[:, b % 2, 0], ALU.subtract).then_inc(S["qr"], 1)
                dve.wait_ge(S["qr"], b + 1)
                v.tensor_copy(qpart[:, b % 2, 1], qr[:]).then_inc(S["qm"], 1)

            def maxima(b, parts):
                for k in parts:
                    i, grp = k // 4, k % 4
                    dve.wait_ge(S["mx"], 8 * b + k + 1)
                    if b >= 1 and k == 0:
                        dve.wait_ge(S["nml"], b)
                    v.tensor_reduce(smax[:, i, 4 * grp:4 * grp + 4],
                                    bank_of["mx", b, k][:, 0:4 * SK].rearrange("p (h k) -> p h k", k=SK),
                                    AX_X, ALU.max).then_inc(S["smax"], 1)

            def neg_max(b):
                dve.wait_ge(S["smax"], 8 * (b + 1))
                if b >= 1:
                    dve.wait_ge(S["nm"], b)
                v.tensor_scalar(nmax[:, :, 0:HEADS], smax[:], -1.0, None, ALU.mult).then_inc(S["nmh"], 1)
                dve.wait_ge(S["nmh"], b + 1)
                v.scalar_tensor_tensor(out=nmax[:, :, HEADS:2 * HEADS], in0=smax[:], scalar=-1.0,
                                       in1=nmax[:, :, 0:HEADS], op0=ALU.mult, op1=ALU.subtract).then_inc(S["nml"], 1)

            def divide(b):
                for i in range(T):
                    n = T * b + i
                    dve.wait_ge(S["oT"], n + 1)
                    heads = bank_of["oT", b, i][:].rearrange("p (h e) -> p h e", e=32)
                    if n >= T:
                        dve.wait_ge(S["onorm"], n - T + 1)
                    v.reciprocal(rden[:, i], heads[:, :, DH]).then_inc(S["rec"], 1)
                    dve.wait_ge(S["rec"], n + 1)
                    if b >= 1:
                        dve.wait_ge(S["aT"], b)
                    v.tensor_tensor(attn[:, i].rearrange("p (h e) -> p h e", e=DH), heads[:, :, 0:DH],
                                    rden[:, i].unsqueeze(2).broadcast_to([P, HEADS, DH]), ALU.mult).then_inc(S["onorm"], 1)

            def residual(b):
                dve.wait_ge(S["wo_ps"], b + 1)
                dve.wait_ge(S["xbias"], b + 1)
                v.tensor_tensor(x_sb[:, b], bank_of["wo", b, 0][:].rearrange("p (i d) -> p i d", i=T),
                                x_sb[:, b], ALU.add).then_inc(S["x2"], 1)
                dve.wait_ge(S["x2"], b + 1)
                moments(b, stats2, mv2, "2")

            def logits(b):
                dve.wait_ge(S["lg_ps"], b + 1)
                v.tensor_tensor(lg[:, T * b:T * b + T],
                                bank_of["lg", b, 0][:, 0:T * NE].rearrange("p (i e) -> p i e", i=T),
                                br_sb[:].unsqueeze(1).broadcast_to([P, T, NE]), ALU.add).then_inc(S["lg"], 1)

            def route(t0, t1):
                n, rt = t1 - t0, s_rt[group(t0)]
                dve.wait_ge(S["lg"], t1 // T)
                dve.wait_ge(S["ident"], 3)
                v.tensor_reduce(lmx[:, t0:t1], lg[:, t0:t1], AX_X, ALU.max).then_inc(rt, 1)
                dve.wait_ge(rt, 1)
                v.tensor_tensor(lgm[:, t0:t1], lg[:, t0:t1], lmx[:, t0:t1].unsqueeze(2).broadcast_to([P, n, NE]),
                                ALU.subtract).then_inc(rt, 1)
                dve.wait_ge(rt, 2)
                v.tensor_scalar(cand[:, t0:t1], lgm[:, t0:t1], 0.0, float(NE), ALU.is_lt, ALU.mult).then_inc(rt, 1)
                dve.wait_ge(rt, 3)
                v.tensor_tensor(cand[:, t0:t1], cand[:, t0:t1], iota_e[:].unsqueeze(1).broadcast_to([P, n, NE]),
                                ALU.add).then_inc(rt, 1)
                dve.wait_ge(rt, 4)
                v.tensor_reduce(idx[:, t0:t1], cand[:, t0:t1], AX_X, ALU.min).then_inc(rt, 1)
                dve.wait_ge(rt, 5)
                v.tensor_tensor(ohg[:, t0:t1], cand[:, t0:t1], idx[:, t0:t1].unsqueeze(2).broadcast_to([P, n, NE]),
                                ALU.is_equal).then_inc(rt, 1)
                dve.wait_ge(rt, 6)

            def gates(t0, t1):
                gt = s_gate[group(t0)]
                dve.wait_ge(s_elg[group(t0)], 1)
                v.tensor_reduce(gate[:, t0:t1], elg[:, t0:t1], AX_X, ALU.add).then_inc(gt, 1)
                dve.wait_ge(gt, 1)
                v.reciprocal(gate[:, t0:t1], gate[:, t0:t1]).then_inc(gt, 1)
                dve.wait_ge(gt, 2)
                if t0 >= RT:
                    v.tensor_tensor(ohg[:, t0:t1], ohg[:, t0:t1], gate[:, t0:t1].unsqueeze(2).broadcast_to([P, t1 - t0, NE]),
                                    ALU.mult).then_inc(gt, 1)
                    dve.wait_ge(gt, 3)

            def sort():
                dve.wait_ge(S["sort_c"], 7)
                dve.wait_ge(S["rank"], 1)
                rank = bank_of["rank", 0, 0][:, 0:(RT + 1) * NE].rearrange("p (t e) -> p t e", e=NE)
                v.tensor_tensor(over[:], rank[:, RT].unsqueeze(2).broadcast_to([P, NE, RT]),
                                iota_rows[:].unsqueeze(1).broadcast_to([P, NE, RT]), ALU.is_gt).then_inc(S["sortd"], 1)
                dve.wait_ge(S["sortd"], 1)
                v.tensor_reduce(tiles_of[:], over[:], AX_X, ALU.add).then_inc(S["sortd"], 1)
                dve.wait_ge(S["sortd"], 2)
                v.tensor_tensor(prefix[:], tiles_of[:].unsqueeze(1).broadcast_to([P, NE, NE]), upto[:],
                                ALU.mult).then_inc(S["sortd"], 1)
                dve.wait_ge(S["sortd"], 3)
                v.tensor_reduce(end_tile[:], prefix[:], AX_X, ALU.add).then_inc(S["sortd"], 1)
                dve.wait_ge(S["sortd"], 4)
                v.tensor_tensor(start_tile[:], end_tile[:], tiles_of[:], ALU.subtract).then_inc(S["st"], 1)
                dve.wait_ge(S["st"], 1)
                v.scalar_tensor_tensor(out=row_e[:], in0=start_tile[:].unsqueeze(1).broadcast_to([P, RT, NE]),
                                       scalar=float(P), in1=rank[:, 0:RT], op0=ALU.mult, op1=ALU.add).then_inc(S["sortd"], 1)
                dve.wait_ge(S["sortd"], 5)
                v.tensor_tensor(row_e[:], row_e[:], ohg[:, 0:RT], ALU.mult).then_inc(S["st"], 1)
                dve.wait_ge(S["st"], 2)
                v.tensor_reduce(row_f[:], row_e[:], AX_X, ALU.add).then_inc(S["sortd"], 1)
                dve.wait_ge(S["sortd"], 6)
                v.tensor_copy(row[:], row_f[:]).then_inc(S["sortd"], 1)
                v.tensor_tensor(past[:], iota_t[0:1].unsqueeze(2).broadcast_to([1, ST, NE]),
                                end_tile[0:1].unsqueeze(1).broadcast_to([1, ST, NE]), ALU.is_ge).then_inc(S["st"], 1)
                dve.wait_ge(S["st"], 3)
                v.tensor_reduce(exp_f[:], past[:], AX_X, ALU.add).then_inc(S["st"], 1)
                dve.wait_ge(S["st"], 4)
                v.tensor_scalar(exp_of[:], exp_f[:], float(NE - 1), None, ALU.min).then_inc(S["exp_of"], 1)

            def expert_of(n):
                return v.value_load(exp_of[0:1, n:n + 1], min_val=0, max_val=NE - 1)

            def take_y(n, e):
                if n >= YRING:
                    dve.wait_ge(s_ys[n % YRING], 16 * (n // YRING))
                dve.wait_ge(S["y"], n + 1)
                v.tensor_tensor(ys[n % YRING].unsqueeze(1), pv_ps[n % 2][:, 0:DM].unsqueeze(1),
                                be_sb[:, bass.ds(e, 1), :], ALU.add).then_inc(S["y_sb"], 1)

            first_moments(0)
            v.memset(probs[64:P], 0.0).then_inc(S["probs_z"], 1)
            for step in STEPS:
                m, f, k = step + MAXI, step + FRONT, step + BACK
                if step == -MAXI:
                    key_parts(1)
                if valid(m):
                    maxima(m, range(0, 4))
                if k == 1:
                    dve.wait_ge(S["router"], 32)
                if step == RB + 1:
                    logits(k - 1)
                    route(0, RT)
                    dve.wait_ge(S["oh_z"], 1)
                    v.tensor_copy(oh[:, 0:RT], ohg[:, 0:RT]).then_inc(S["oh"], 1)
                if valid(k):
                    divide(k)
                if valid(m):
                    maxima(m, range(4, 8))
                    neg_max(m)
                if valid(f + 1):
                    first_moments(f + 1)
                if valid(f):
                    query_parts(f)
                if f == 0:
                    key_parts(0)
                    dve.wait_ge(S["kl"], 1)
                    v.memset(zeros, 0.0).then_inc(S["zeros"], 1)
                if valid(k - 1) and step != RB + 1:
                    logits(k - 1)
                if step == RB + 1:
                    sort()
                if valid(k):
                    residual(k)
                if step == -2:
                    dve.wait_ge(S["bvo"], 1)
                    dve.wait_ge(S["bo"], 16)
                    v.tensor_tensor(bo_sb[:], bank_of["bvo", 0, 0][:, 0:DM], bo_sb[:], ALU.add).then_inc(S["bo2"], 1)

            def add_bias(t, e):
                if e:
                    dve.wait_ge(s_biased[t - RT], e)
                if t == RT and e == 0:
                    dve.wait_ge(S["acc"], NE)
                y = x_sb[:, t // T, t % T]
                v.scalar_tensor_tensor(out=y, in0=be_sb[:, e], scalar=ohg[:, t, e:e + 1], in1=y,
                                       op0=ALU.mult, op1=ALU.add).then_inc(s_biased[t - RT], 1)

            def add_products(g):
                t = RT + g // G
                y = x_sb[:, t // T, t % T]
                dve.wait_ge(S["all"], g + 1)
                for i in range(2):
                    e = 2 * (g % G) + i
                    if e == 0 and t > RT:
                        dve.wait_ge(s_biased[t - RT], NE)
                    elif e > 0:
                        dve.wait_ge(S["acc"], 2 * g + i)
                    v.scalar_tensor_tensor(out=y, in0=bank_of["all", g, 0][:, i * DM:(i + 1) * DM],
                                           scalar=ohg[:, t, e:e + 1], in1=y,
                                           op0=ALU.mult, op1=ALU.add).then_inc(S["acc"], 1)
                    for b in biases_at(("all", g, 0))[i:i + 1]:
                        add_bias(*b)

            def combine(t):
                y = x_sb[:, t // T, t % T]
                dve.wait_ge(s_back[t // T], 16 * T)
                v.scalar_tensor_tensor(out=y, in0=xn2[:, t // T, t % T], scalar=gate[:, t:t + 1], in1=y,
                                       op0=ALU.mult, op1=ALU.add).then_inc(S["comb"], 1)

            combined = iter(range(RT))
            dve.wait_ge(S["be"], 16 * NE)
            dve.wait_ge(S["exp_of"], 1)
            for j in TAIL:
                kind, n, i = j
                if kind == "oT" and i == T - 1:
                    divide(n)
                elif kind == "lg":
                    logits(n)
                    route(T * n, T * n + T)
                    gates(T * n, T * n + T)
                elif kind == "wo":
                    residual(n)
                elif kind == "tile":
                    e = next_e if n else expert_of(0)
                    take_y(n, e)
                    if n + 1 < ST:
                        next_e = expert_of(n + 1)
                    if n == 0:
                        gates(0, RT)
                    for b in biases_at(j):
                        add_bias(*b)
                elif kind == "all":
                    add_products(n)
                    if n >= 2 * G * T - RB:
                        for _ in range(2):
                            combine(next(combined))

        @block.tensor
        def _(pe):
            m_ = nc.tensor.matmul
            transpose = nc.tensor.transpose
            pe.wait_ge(S["ident"], 3)
            for n in range(4):
                half, c = n // 2, n % 2
                pe.wait_ge(s_ctx[half], 16)
                for b in range(HB):
                    last = transpose(early[n][0:DCC, b * SK:(b + 1) * SK],
                                     ctx_sb[:, half * HB + b, c * DCC:(c + 1) * DCC], ident[0:SK, 0:SK])
                last.then_inc(S["ctxT"], 1)

            def keys(half):
                pe.wait_ge(S["ctxT_sb"], 2 * (half + 1))
                for m in range(C):
                    for c in range(CC):
                        last = m_(early[C * half + m][:, 0:HB * SK], wk_sb[:, c, m * P:(m + 1) * P],
                                  ctxT[:, c, half_keys(half)], start=(c == 0), stop=(c == CC - 1))
                    last.then_inc(S["kT"], 1)

            def job(j):
                kind, b, k = j
                dst = bank_of[j]
                if before[j] is not None:
                    pe.wait_ge(*freed_by(before[j]))
                if kind == "xT":
                    pe.wait_ge(S["xn1"], T * (b + 1))
                    for c in range(C):
                        for i in range(T):
                            last = transpose(dst[:, c * SQ + i * P:c * SQ + (i + 1) * P],
                                             xn[:, i, c * P:(c + 1) * P], ident[:])
                    last.then_inc(S["xT"], 1)
                elif kind == "q":
                    if b == 0:
                        pe.wait_ge(S["wq"], 16)
                    pe.wait_ge(S["xT_sb"], b + 1)
                    for m in range(C):
                        for c in range(C):
                            last = m_(dst[:, m * SQ:(m + 1) * SQ], wq_sb[:, c, m * P:(m + 1) * P],
                                      xnT[:, c, :], start=(c == 0), stop=(c == C - 1))
                    last.then_inc(S["q"], 1)
                elif kind == "v":
                    if b == 0:
                        pe.wait_ge(S["wv"], 16)
                        pe.wait_ge(S["ctxT_sb"], 4)
                    for c in range(CC):
                        last = m_(dst[0:SK, 0:DM], ctxT[:, c, b * SK:(b + 1) * SK], wv_sb[:, c, :],
                                  start=(c == 0), stop=(c == CC - 1))
                    last.then_inc(S["v"], 1)
                elif kind == "bvo":
                    pe.wait_ge(S["bvb"], 1)
                    pe.wait_ge(S["wo"], 16)
                    for c in range(C):
                        last = m_(dst[:, 0:DM], bv_bc[:, c], wo_sb[:, c], start=(c == 0), stop=(c == C - 1))
                    last.then_inc(S["bvo"], 1)
                elif kind == "mx":
                    i, h0 = k // 4, 4 * (k % 4)
                    pe.wait_ge(s_qrd[b % QRING], 16 * NBLK * (b // QRING + 1))
                    for j4 in range(4):
                        last = m_(dst[:, j4 * SK:(j4 + 1) * SK], qst[0:NBLK * DH, b % QRING, h0 + j4, i * P:(i + 1) * P],
                                  kst[0:NBLK * DH, h0 + j4, b * SK:(b + 1) * SK], start=True, stop=True)
                    last.then_inc(S["mx"], 1)
                elif kind == "nm":
                    pe.wait_ge(S["nml"], b + 1)
                    d = dst[0:2 * HEADS, 0:P].bitcast(BF16)
                    for i in range(T):
                        last = transpose(d[:, i * P:(i + 1) * P], nmax[:, i, :], identb[:])
                    last.then_inc(S["nm"], 1)
                elif kind == "oT":
                    pe.wait_ge(S["pv_sb"], 2 * (b + 1))
                    for q in range(4):
                        last = transpose(dst[:, q * P:(q + 1) * P], rawT[:, q, k * P:(k + 1) * P], ident[:])
                    last.then_inc(S["oT"], 1)
                elif kind == "aT":
                    pe.wait_ge(S["onorm"], T * (b + 1))
                    for c in range(C):
                        for i in range(T):
                            last = transpose(dst[:, c * SQ + i * P:c * SQ + (i + 1) * P],
                                             attn[:, i, c * P:(c + 1) * P], ident[:])
                    last.then_inc(S["aT"], 1)
                elif kind == "wo":
                    pe.wait_ge(S["aT_sb"], b + 1)
                    for i in range(T):
                        for c in range(C):
                            last = m_(dst[:, i * DM:(i + 1) * DM], attnT[:, c, i * P:(i + 1) * P], wo_sb[:, c, :],
                                      start=(c == 0), stop=(c == C - 1))
                    last.then_inc(S["wo_ps"], 1)
                elif kind == "x2T":
                    pe.wait_ge(S["xn2"], T * (b + 1))
                    for c in range(C):
                        for i in range(T):
                            last = transpose(dst[:, c * SQ + i * P:c * SQ + (i + 1) * P],
                                             xn2[:, b, i, c * P:(c + 1) * P], ident[:])
                    last.then_inc(S["x2T"], 1)
                elif kind == "all":
                    if b == 0:
                        pe.wait_ge(S["we"], 16 * NE)
                    t, e2 = RT + b // G, b % G
                    for c in range(C):
                        last = m_(dst[:], xn2T[:, c, t // T % 2, t % T * P:(t % T + 1) * P],
                                  we_sb[:, c, 2 * e2:2 * e2 + 2, :].rearrange("p e n -> p (e n)"),
                                  start=(c == 0), stop=(c == C - 1))
                    last.then_inc(S["all"], 1)
                elif kind == "rank":
                    pe.wait_ge(S["oh"], 1)
                    m_(dst[:, 0:(RT + 1) * NE], before_me[:], oh[:].rearrange("p t e -> p (t e)"), start=True, stop=False)
                    for t in range(RT):
                        last = m_(dst[:, (t + 1) * NE:(RT + 1) * NE], all_ones[:],
                                  oh[:, t].unsqueeze(1).broadcast_to([P, RT - t, NE]), start=False, stop=(t == RT - 1))
                    last.then_inc(S["rank"], 1)
                else:
                    pe.wait_ge(S["x2T_sb"], b + 1)
                    for i in range(T):
                        for c in range(C):
                            last = m_(dst[:, i * NE:(i + 1) * NE], xn2T[:, c, b % 2, i * P:(i + 1) * P],
                                      wr_sb[:, c, :], start=(c == 0), stop=(c == C - 1))
                    last.then_inc(S["lg_ps"], 1)

            def scores(b, u):
                n = U * b + u
                if n >= 2:
                    pe.wait_ge(S["exp"], n - 1)
                if u == 0:
                    pe.wait_ge(S["nmrow"], 32 * (b + 1))
                for r in range(2):
                    last = m_(s_ps[n % 2][0:SK, r * SQ:(r + 1) * SQ], kst[:, 2 * u + r, b * SK:(b + 1) * SK],
                              qst[:, b % QRING, 2 * u + r, :], start=True, stop=True)
                last.then_inc(S["scores"], 1)

            def weighted(g):
                b, q = g // 4, g % 4
                pe.wait_ge(S["exp"], 2 * g + 2)
                if g >= 4:
                    pe.wait_ge(S["pv_sb"], g // 2 - 1)
                for j in range(4):
                    last = m_(pv_ps[q // 2][32 * j:32 * j + 32, (q % 2) * SQ:(q % 2 + 1) * SQ], vaug[:, b, 4 * q + j, :],
                              probs[:, (2 * g + j // 2) % 4, j % 2, :], start=True, stop=True)
                last.then_inc(S["pv"], 1)

            def turn(n):
                pe.wait_ge(s_xs[n % XRING], 16 * (n // XRING + 1))
                if n >= 2:
                    pe.wait_ge(S["xsT_sb"], n - 1)
                for c in range(C):
                    last = transpose(s_ps[n % 2][:, c * P:(c + 1) * P],
                                     xs[n % XRING][:, c * P:(c + 1) * P], ident[:])
                last.then_inc(S["xsT"], 1)

            def expert(n, e):
                pe.wait_ge(S["xsT_sb"], n + 1)
                if n >= 2:
                    pe.wait_ge(S["y_sb"], n - 1)
                for c in range(C):
                    last = m_(pv_ps[n % 2][:, 0:DM], xsT[n % 2][:, c * P:(c + 1) * P],
                              we_sb[:, c, bass.ds(e, 1), :], start=(c == 0), stop=(c == C - 1))
                last.then_inc(S["y"], 1)

            for step in STEPS:
                if step == 1 - FRONT:
                    pe.wait_ge(S["wk"], 16)
                    keys(0)
                if step == -MAXI:
                    keys(1)
                    pe.wait_ge(s_krd[0], 16 * NBLK)
                if step == HB - MAXI:
                    pe.wait_ge(s_krd[1], 16 * NBLK)
                if step == 0:
                    pe.wait_ge(S["kst_ones"], 1)
                    pe.wait_ge(S["router"], 32)
                for u in range(U):
                    if valid(step):
                        scores(step, u)
                    g = 4 * step + u // 2 - 1
                    if u % 2 == 0 and 0 <= g < 4 * B:
                        weighted(g)
                    for j in jobs_at(step, u):
                        job(j)
            weighted(4 * B - 1)
            for j in TAIL:
                kind, n, _ = j
                if kind != "tile":
                    job(j)
                    continue
                if n == 0:
                    pe.wait_ge(S["exp_of"], 1)
                    pe.wait_ge(S["exp"], U * B)
                    pe.wait_ge(S["pv_sb"], 2 * B)
                    turn(0)
                e = nc.tensor.value_load(exp_of[0:1, n:n + 1], min_val=0, max_val=NE - 1)
                if n + 1 < ST:
                    turn(n + 1)
                expert(n, e)


_INS = ['x', 'ctx_768', 'L0_xattn_Wq', 'L0_xattn_bq', 'L0_xattn_Wk', 'L0_xattn_bk', 'L0_xattn_Wv', 'L0_xattn_bv',
        'L0_xattn_Wo', 'L0_xattn_bo', 'L0_ffn_router_w', 'L0_ffn_router_b', 'L0_ffn_expert_w', 'L0_ffn_expert_b']
_OUTS = [((8, 256, 256), 'float32')]


def kernel(**inputs):
    import numpy as _np
    import concourse.bacc as _bacc
    from concourse import mybir as _mybir
    from concourse.bass_utils import run_bass_kernel_spmd as _run

    nc = _bacc.Bacc("TRN2", target_bir_lowering=False, num_devices=1)
    arrays, args = {}, []
    for name in _INS:
        a = _np.ascontiguousarray(inputs[name])
        arrays[f"in_{name}_dram"] = a
        args.append(nc.dram_tensor(f"in_{name}_dram", a.shape, _mybir.dt.from_np(a.dtype), kind="ExternalInput").ap())
    for i, (shape, dtype) in enumerate(_OUTS):
        dt = _mybir.dt.from_np(_np.dtype(dtype))
        args.append(nc.dram_tensor(f"out_{i}_dram", shape, dt, kind="ExternalOutput").ap())
    xattn_moe_kernel(nc, *args)
    r = _run(nc, [arrays], core_ids=[0])
    got = tuple(r.results[0][f"out_{i}_dram"] for i in range(len(_OUTS)))
    return got[0]
```
